# Optimizing a Trainium2 kernel written in Bass

```python
import numpy as np
import jax
import jax.numpy as jnp

def _softmax(x, axis=-1):
    return jax.nn.softmax(x, axis=axis)

def _gelu(x):
    return jax.nn.gelu(x, approximate=True)

def _silu(x):
    return jax.nn.silu(x)

def _sigmoid(x):
    return jax.nn.sigmoid(x)

def _layernorm(x, axis=-1, eps=1e-05):
    m = jnp.mean(x, axis=axis, keepdims=True)
    v = jnp.var(x, axis=axis, keepdims=True)
    return (x - m) / jnp.sqrt(v + eps)

def _scatter_add(tgt, idx, src, axis=0):
    return tgt.at[idx].add(src)

def _segment_sum(src, seg, n):
    return jax.ops.segment_sum(src, seg, n)
kernel_name = 'mk_seq_postln_d1_jaxref_r8_d86d16'

def setup_inputs(seed: int=0):
    np.random.seed(seed)
    _w = jnp.asarray

    def _L0_attn_setup():
        import jax, jax.numpy as jnp
        import numpy as np
        B, S, D_IN, D_H = (8, 512, 128, 128)

        def _uniform(k, shape, bound):
            return jax.random.uniform(k, shape, jnp.float32, -bound, bound)

        def log_g(v):
            return jnp.where(v >= 0, jnp.log(jnp.where(v >= 0, v + 0.5, 1.0)), -jax.nn.softplus(-v))
        key = jax.random.key(seed)
        ks = jax.random.split(key, 5)
        stdv = 1.0 / np.sqrt(D_IN)
        x = jax.random.normal(ks[0], (B, S, D_IN), jnp.float32)
        Wz = _uniform(ks[1], (D_H, D_IN), stdv)
        bz = _uniform(ks[2], (D_H,), stdv)
        Wh = _uniform(ks[3], (D_H, D_IN), stdv)
        bh = _uniform(ks[4], (D_H,), stdv)
        return {'x': x, 'Wz': Wz, 'bz': bz, 'Wh': Wh, 'bh': bh}
    _L0_attn_in = _L0_attn_setup()

    def _L0_ffn_setup():
        import jax, jax.numpy as jnp
        import numpy as np
        B, T, E, C, H, G = (2, 256, 8, 128, 256, 16)
        key = jax.random.key(seed)
        ks = jax.random.split(key, 7)
        return {'hidden_states': jax.random.normal(ks[0], (B, T, C), jnp.float32), 'w_red': jax.random.normal(ks[1], (C, G), jnp.float32) * 0.02, 'wg': jax.random.normal(ks[2], (E, G), jnp.float32), 'W1': jax.random.normal(ks[3], (E, C, H), jnp.float32) * 0.02, 'b1': jax.random.normal(ks[4], (E, H), jnp.float32) * 0.02, 'W2': jax.random.normal(ks[5], (E, H, C), jnp.float32) * 0.02, 'b2': jax.random.normal(ks[6], (E, C), jnp.float32) * 0.02}
    _L0_ffn_in = _L0_ffn_setup()
    _d = {'L0_attn_x': _L0_attn_in['x'], 'L0_attn_Wz': _L0_attn_in['Wz'], 'L0_attn_bz': _L0_attn_in['bz'], 'L0_attn_Wh': _L0_attn_in['Wh'], 'L0_attn_bh': _L0_attn_in['bh'], 'L0_ffn_w_red': _L0_ffn_in['w_red'], 'L0_ffn_wg': _L0_ffn_in['wg'], 'L0_ffn_W1': _L0_ffn_in['W1'], 'L0_ffn_b1': _L0_ffn_in['b1'], 'L0_ffn_W2': _L0_ffn_in['W2'], 'L0_ffn_b2': _L0_ffn_in['b2']}
    _x0 = _d['L0_attn_x']
    _d['L0_attn_x'] = jax.random.normal(jax.random.fold_in(jax.random.key(seed), 1), (8, 512, 128), dtype=_x0.dtype)
    del _x0
    return _d

def reference(L0_attn_x, L0_attn_Wz, L0_attn_bz, L0_attn_Wh, L0_attn_bh, L0_ffn_w_red, L0_ffn_wg, L0_ffn_W1, L0_ffn_b1, L0_ffn_W2, L0_ffn_b2):

    def _L0_attn_ref(x, Wz, bz, Wh, bh):
        import jax, jax.numpy as jnp
        import numpy as np
        B, S, D_IN, D_H = (8, 512, 128, 128)

        def _uniform(k, shape, bound):
            return jax.random.uniform(k, shape, jnp.float32, -bound, bound)

        def log_g(v):
            return jnp.where(v >= 0, jnp.log(jnp.where(v >= 0, v + 0.5, 1.0)), -jax.nn.softplus(-v))
        k = jnp.einsum('bsd,hd->bsh', x, Wz) + bz
        log_z = -jax.nn.softplus(-k)
        log_coeffs = -jax.nn.softplus(k)
        pre = jnp.einsum('bsd,hd->bsh', x, Wh) + bh
        log_tilde_h = log_g(pre)
        log_h0 = jnp.full((x.shape[0], 1, Wh.shape[0]), jnp.log(0.5), x.dtype)
        log_b = jnp.concatenate([log_h0, log_z + log_tilde_h], axis=1)
        a_star = jnp.pad(jnp.cumsum(log_coeffs, axis=1), ((0, 0), (1, 0), (0, 0)))
        log_x = a_star + jax.lax.cumlogsumexp(log_b - a_star, axis=1)
        h = jnp.exp(log_x)
        return h[:, 1:]

    def _L0_ffn_ref(hidden_states, w_red, wg, W1, b1, W2, b2):
        import jax, jax.numpy as jnp
        import numpy as np
        B, T, E, C, H, G = (2, 256, 8, 128, 256, 16)
        b, t, c = hidden_states.shape
        x = hidden_states.reshape(-1, c)
        x_red = x @ w_red
        wg_n = wg / jnp.maximum(jnp.linalg.norm(wg, axis=1, keepdims=True), 0.0001)
        logits = x_red @ wg_n.T
        gates = jax.nn.softmax(logits, axis=1)
        scores = jnp.max(gates, axis=1)
        idx = jnp.argmax(gates, axis=1)
        h = jnp.einsum('nc,ech->neh', x, W1) + b1[None]
        h = jnp.take_along_axis(h, idx[:, None, None], axis=1)[:, 0, :]
        h = jax.nn.gelu(h, approximate=False)
        o = jnp.einsum('nh,ehc->nec', h, W2) + b2[None]
        o = jnp.take_along_axis(o, idx[:, None, None], axis=1)[:, 0, :]
        o = o * scores[:, None]
        return o.reshape(b, t, c)
    x = L0_attn_x
    x = _layernorm(x + _L0_attn_ref(x, L0_attn_Wz, L0_attn_bz, L0_attn_Wh, L0_attn_bh), axis=-1)
    x = _layernorm(x + _L0_ffn_ref(x, L0_ffn_w_red, L0_ffn_wg, L0_ffn_W1, L0_ffn_b1, L0_ffn_W2, L0_ffn_b2), axis=-1)
    return x

_drawn_inputs = setup_inputs


def setup_inputs(seed=0):
    import zlib

    import numpy as np

    out = dict(_drawn_inputs(seed))
    spreads = {}
    factors = {'L0_attn_bz': 8.0,
     'L0_ffn_w_red': 8.0,
     'L0_ffn_wg': 8.0,
     'L0_ffn_W1': 8.0,
     'L0_ffn_b1': 8.0,
     'L0_ffn_W2': 8.0,
     'L0_ffn_b2': 8.0}
    for name, (base, spread) in spreads.items():
        noise = np.random.default_rng([zlib.crc32(name.encode()), seed]).standard_normal(out[name].shape)
        drawn = base * np.exp(spread * noise) if base else spread * noise
        out[name] = jnp.asarray(drawn.astype(out[name].dtype))
    for name, factor in factors.items():
        out[name] = (out[name] * factor).astype(out[name].dtype)
    return out
```

```python
import concourse.bass as bass
from concourse import mybir
from contextlib import ExitStack

B, S, C = 8, 512, 128
E, H, R = 8, 256, 16
P = 128
N = B * S
TB = S // P
G = 2
BG = B // G
TG = BG * TB
NG = TG * P
SG = 2 * -(-((NG + E * (P - 1)) // P) // 2)
QG = SG // 2
Q = G * QG
LN_EPS = 1e-5
NORM_MIN = 1e-4

CF_IDENT = 0
CF_DESC = CF_IDENT + P
CF_RESET = CF_DESC + TG * E
CF_TILE = CF_RESET + TG * E
CF_BASE = CF_TILE + TG * SG
CF_TILE_E = CF_BASE + TG * SG
CF_PART = CF_TILE_E + SG * E
CF_END = CF_PART + 1
CB_BEFORE = 0
CB_ONES = CB_BEFORE + P
CB_SLOT = CB_ONES + P
CB_END = CB_SLOT + P


def build_mingru_top1_moe(nc, xT_d, wzT_d, whT_d, bz_d, bh_d, wredT_d, wgT_d, w1_d, b1_d, w2_d, b2_d, cf_d, cb_d, out_d):
    f32, bf16, i32, u32 = mybir.dt.float32, mybir.dt.bfloat16, mybir.dt.int32, mybir.dt.uint32
    ALU = mybir.AluOpType
    ACT = mybir.ActivationFunctionType
    AX = mybir.AxisListType

    x1_dram = [nc.dram_tensor(f"x1_rows_{g}", (NG, C), f32).ap() for g in range(G)]
    o_dram = [nc.dram_tensor(f"expert_out_rows_{g}", (SG * P, C), f32).ap() for g in range(G)]
    bias_dram = nc.dram_tensor("bias_parts", (3, E * H + E * C), bf16).ap()

    ctx = ExitStack()
    with ctx:
        def sb(name, shape, dt=f32):
            return ctx.enter_context(nc.sbuf_tensor(name, shape, dt))

        def sem(name):
            return ctx.enter_context(nc.semaphore(name))

        RING, RING4 = 2, 4
        xT = sb("xT", [P, N])
        wz = sb("wz", [P, C])
        wh = sb("wh", [P, C])
        gate_bias = sb("gate_bias", [P, 4])
        cf = sb("cf", [P, CF_END])
        cb = sb("cb", [P, CB_END], bf16)
        w1 = sb("w1", [P, E * H])
        w2 = sb("w2", [P, E, H // P, C])
        keep = sb("keep", [P, RING, S])
        z = sb("z", [P, RING, S])
        sg = sb("sg", [P, RING, S])
        cand = sb("cand", [P, RING, S])
        zcand = sb("zcand", [P, RING, S])
        h = sb("h", [P, RING4, S])
        sT = sb("sT", [P, RING4, S])
        st1 = sb("st1", [P, RING, TB, 6])
        mv = sb("mv", [P, B * TB, 2])
        var1 = sb("var1", [P, B * TB])
        rstd = sb("rstd", [P, B * TB])
        nmean = sb("nmean", [P, B * TB])
        nmr = sb("nmr", [P, B * TB])
        x1 = sb("x1", [P, B * TB, C])
        wredT = sb("wredT", [R, C])
        wredc = sb("wredc", [R, C])
        wgT = sb("wgT", [R, E])
        rtmp = sb("rtmp", [R, 6 * E])
        ones16 = sb("ones16", [R, R])
        half = sb("half", [P, 2 * TG])
        router = sb("router", [P, E])
        braw = sb("braw", [P, 24])
        brem = sb("brem", [P, 2, 24])
        bpart = sb("bpart", [P, 3, 24], bf16)
        bias3 = sb("bias3", [3, E * H + E * C], bf16)
        mx = sb("mx", [P, TG])
        gap = sb("gap", [P, G, TG, E])
        key = sb("key", [P, TG, E])
        kmx = sb("kmx", [P, TG])
        oh = sb("oh", [P, E, TG], bf16)
        incl = sb("incl", [P, E, TG], bf16)
        cnt = sb("cnt", [P, 2, E], i32)
        ends = sb("ends", [P, E])
        base = sb("base", [P, E])
        posx = sb("posx", [P, E, TG])
        slot = sb("slot", [P, G, TG], u32)
        lane = sb("lane", [P, 2, TG], u32)
        lanef = sb("lanef", [P, TG])
        ohB = sb("ohB", [P, TG, P], bf16)
        ohA = sb("ohA", [P, TG, SG])
        rhsA = sb("rhsA", [P, TG, 2, SG], bf16)
        tlow = sb("tlow", [P, SG])
        gidx = sb("gidx", [P, G, SG], u32)
        tcmp = sb("tcmp", [P, SG, E])
        tsum = sb("tsum", [P, SG])
        texp = sb("texp", [P, G, SG], i32)
        sgap = sb("sgap", [P, TG, E])
        sp_ = sb("sp_", [P, TG, E])
        sn_ = sb("sn_", [P, TG, E])
        rn_ = sb("rn_", [P, TG, E])
        den = sb("den", [P, TG])
        score = sb("score", [P, G, TG])
        xg = sb("xg", [P, Q * 2, C])
        xgT = sb("xgT", [P, RING, 2 * P])
        hg = sb("hg", [P, RING, 2 * H])
        hgT = sb("hgT", [P, RING, 2, H // P, P])
        osb = sb("osb", [P, Q, 2 * C])
        og = sb("og", [P, B * TB, C])
        st2 = sb("st2", [P, B * TB, 6])
        mv2 = sb("mv2", [P, B * TB, 2])
        var2 = sb("var2", [P, B * TB])
        rstd2 = sb("rstd2", [P, B * TB])
        y = og

        bank = [ctx.enter_context(nc.psum_tensor(f"bank{i}", [P, 512], f32)) for i in range(8)]
        k_ps, pre_ps, s_ps = bank[0:2], bank[2:4], bank[4:6]
        logit_ps, route_ps = bank[6], bank[7]
        xT_ps, h_ps, hT_ps, o_ps = bank[0:2], bank[2:4], bank[4:6], bank[6:8]
        RANK, COUNT, TABLE = 0, 128, 160

        ld_gate, ld_rt, ld_cf, ld_cb, ld_w1, ld_w2, ld_b = (sem(n) for n in (
            "gate_weights_loaded", "router_weights_loaded", "constants_loaded", "bf16_constants_loaded",
            "w1_loaded", "w2_loaded", "biases_loaded"))
        ld_x = [sem(f"x_loaded_{s}") for s in range(B)]
        gbias_ready = sem("gate_bias_ready")
        half_ready = sem("half_ready")
        rt_dve, rt_pe, rt_pool = sem("router_dve"), sem("router_pe"), sem("router_pool")
        router_ready = sem("router_ready")
        bsplit, bstored, bias_ready = sem("bias_split"), sem("bias_stored"), sem("bias_loaded")
        k_done, pre_done = sem("k_done"), sem("pre_done")
        z_done, keep_done, sg_done = sem("z_done"), sem("keep_done"), sem("sg_done")
        cand_done, zcand_done, h_done = sem("cand_done"), sem("zcand_done"), sem("h_done")
        s_done, stok_done, logit_done = sem("s_done"), sem("s_tokens_done"), sem("logits_done")
        st_done, mv_done = sem("stats_done"), sem("mean_var_done")
        pool_ln, rstd_done, x1_done = sem("pool_ln_chain"), sem("rstd_done"), sem("x1_done")
        x1_stored = [sem(f"x1_stored_{g}") for g in range(G)]
        gap_done = sem("gap_done")
        rc = sem("route_chain")
        incl_done, rank_done, table_ready, table_done = sem("incl_done"), sem("rank_done"), sem("table_ready"), sem("table_done")
        gidx_done, texp_done = sem("gather_index_done"), sem("tile_expert_done")
        slot_done = sem("slot_done")
        sgap_done, sig_done, score_done = sem("score_gap_done"), sem("score_sigmoids_done"), sem("score_done")
        sc = sem("score_chain")
        xg_done = [sem(f"x_gathered_{i}") for i in range(2)]
        xT_done, xgT_done, up_done, gelu_done = sem("x_transposed"), sem("xgT_copied"), sem("up_done"), sem("gelu_done")
        hT_done, hgT_done, down_done, o_done = sem("h_transposed"), sem("hgT_copied"), sem("down_done"), sem("o_copied")
        o_stored = [sem(f"o_stored_{g}") for g in range(G)]
        og_done = [sem(f"o_gathered_{i}") for i in range(4)]
        res_done, st2_done, mv2_done, rstd2_done = sem("residual_done"), sem("stats2_done"), sem("mean_var2_done"), sem("rstd2_done")
        pool_ln2 = sem("pool_ln2_chain")
        y_done, out_stored = sem("y_done"), sem("out_stored")

        LAG = 2
        tok = lambda s: slice(s * S, (s + 1) * S)
        tiles = lambda s: slice(s * TB, (s + 1) * TB)

        COMBINE_AFTER = [QG + 4, QG + 6, QG + 8, QG + 10]

        block = ctx.enter_context(nc.Block())

        @block.sync
        def _(sp):
            sp.dma_start(wz[:, :], wzT_d).then_inc(ld_gate, 16)
            sp.dma_start(xT[:, tok(0)], xT_d[:, tok(0)]).then_inc(ld_x[0], 16)
            sp.dma_start(wh[:, :], whT_d).then_inc(ld_gate, 16)
            sp.dma_start(gate_bias[:, 0:1], bz_d).then_inc(ld_gate, 16)
            sp.dma_start(gate_bias[:, 1:2], bh_d).then_inc(ld_gate, 16)
            sp.dma_start(xT[:, tok(1)], xT_d[:, tok(1)]).then_inc(ld_x[1], 16)
            sp.dma_start(wredT[:, :], wredT_d).then_inc(ld_rt, 16)
            sp.dma_start(wgT[:, :], wgT_d).then_inc(ld_rt, 16)
            sp.dma_start(cf[:, :], cf_d).then_inc(ld_cf, 16)
            for s in range(2, 5):
                sp.dma_start(xT[:, tok(s)], xT_d[:, tok(s)]).then_inc(ld_x[s], 16)
            sp.dma_start(cb[:, :], cb_d).then_inc(ld_cb, 16)
            sp.dma_start(braw[:, 0:16], b1_d.rearrange("e h -> (e h)").rearrange("(p f) -> p f", p=P)).then_inc(ld_b, 16)
            sp.dma_start(braw[:, 16:24], b2_d.rearrange("e h -> (e h)").rearrange("(p f) -> p f", p=P)).then_inc(ld_b, 16)
            for s in range(5, B):
                sp.dma_start(xT[:, tok(s)], xT_d[:, tok(s)]).then_inc(ld_x[s], 16)
            sp.dma_start(w1[:, :].rearrange("c (e h) -> c e h", e=E), w1_d.rearrange("e c h -> c e h")).then_inc(ld_w1, 16)
            sp.dma_start(w2[:, :, :, :], w2_d.rearrange("e (k p) c -> p e k c", p=P)).then_inc(ld_w2, 16)
            sp.wait_ge(bsplit, 5)
            sp.dma_start(bias_dram[:, 0:E * H].rearrange("k (p f) -> p k f", p=P), bpart[:, :, 0:16]).then_inc(bstored, 16)
            sp.dma_start(bias_dram[:, E * H:].rearrange("k (p f) -> p k f", p=P), bpart[:, :, 16:24]).then_inc(bstored, 16)
            sp.wait_ge(bstored, 32)
            sp.dma_start(bias3[:, :], bias_dram).then_inc(bias_ready, 16)
            for s in range(B):
                g, t0 = s // BG, (s % BG) * TB
                sp.wait_ge(x1_done, s + 1)
                sp.dma_start(x1_dram[g][t0 * P:(t0 + TB) * P, :].rearrange("(t p) c -> p t c", p=P),
                             x1[:, tiles(s), :]).then_inc(x1_stored[g], 16)

            def store_pair(q):
                g, a = q // QG, 2 * (q % QG)
                sp.wait_ge(o_done, q + 1)
                sp.dma_start(o_dram[g][a * P:(a + 2) * P, :].rearrange("(t p) c -> p t c", p=P),
                             osb[:, q, :].rearrange("p (t c) -> p t c", t=2)).then_inc(o_stored[g], 16)

            def store_out(s):
                sp.wait_ge(y_done, s + 1)
                sp.dma_start(out_d[s * S:(s + 1) * S, :].rearrange("(t p) c -> p t c", p=P),
                             y[:, tiles(s), :]).then_inc(out_stored, 16)

            for q in range(Q):
                store_pair(q)
                if q - 1 in COMBINE_AFTER:
                    store_out(COMBINE_AFTER.index(q - 1))
            for s in range(BG, B):
                store_out(s)
            sp.wait_ge(out_stored, 16 * B)

        @block.tensor
        def _(pe):
            ident = cf[:, CF_IDENT:CF_IDENT + P]

            def gates(s):
                if s == 0:
                    pe.wait_ge(ld_gate, 64)
                pe.wait_ge(ld_x[s], 16)
                if s >= 2:
                    pe.wait_ge(z_done, s - 1)
                nc.tensor.matmul(k_ps[s % 2][:, :], wz[:, :], xT[:, tok(s)], start=True, stop=True).then_inc(k_done, 1)
                if s >= 2:
                    pe.wait_ge(cand_done, s - 1)
                nc.tensor.matmul(pre_ps[s % 2][:, :], wh[:, :], xT[:, tok(s)], start=True, stop=True).then_inc(pre_done, 1)

            def router_weights():
                pe.wait_ge(rt_dve, 1)
                nc.tensor.matmul(route_ps[0:R, 0:E], ones16[:, :], rtmp[:, 0:E], start=True, stop=True).then_inc(rt_pe, 1)
                pe.wait_ge(rt_dve, 7)
                nc.tensor.matmul(route_ps[:, 0:E], wredc[:, :], rtmp[:, 3 * E:4 * E], start=True, stop=True).then_inc(rt_pe, 1)

            def tokens(s):
                pe.wait_ge(s_done, s + 1)
                if s == 0:
                    pe.wait_ge(ld_cf, 16)
                if s >= 2:
                    pe.wait_ge(x1_done, s - 1)
                for j in range(TB):
                    last = nc.tensor.transpose(s_ps[s % 2][:, j * P:(j + 1) * P], sT[:, s % RING4, j * P:(j + 1) * P], ident)
                last.then_inc(stok_done, 1)
                if s == 0:
                    pe.wait_ge(router_ready, 1)
                if s % BG == 0 and s:
                    pe.wait_ge(gap_done, s // BG)
                for j in range(TB):
                    t = (s % BG) * TB + j
                    last = nc.tensor.matmul(logit_ps[:, t * E:(t + 1) * E], sT[:, s % RING4, j * P:(j + 1) * P],
                                            router[:, :], start=True, stop=True)
                last.then_inc(logit_done, 1)

            def rank(g):
                pe.wait_ge(incl_done, g + 1)
                if g == 0:
                    pe.wait_ge(ld_cb, 16)
                if g:
                    pe.wait_ge(gidx_done, g)
                flat_oh = oh[:, :, :].rearrange("p e t -> p (e t)")
                flat_incl = incl[:, :, :].rearrange("p e t -> p (e t)")
                nc.tensor.matmul(route_ps[:, RANK:RANK + E * TG], cb[:, CB_BEFORE:CB_BEFORE + P], flat_oh, start=True, stop=False)
                nc.tensor.matmul(route_ps[:, RANK:RANK + E * TG], cb[:, CB_ONES:CB_ONES + P], flat_incl, start=False, stop=True)
                nc.tensor.matmul(route_ps[:, COUNT:COUNT + E], cb[:, CB_ONES:CB_ONES + P], incl[:, :, TG - 1],
                                 start=True, stop=True).then_inc(rank_done, 1)

            def table(g):
                pe.wait_ge(table_ready, g + 1)
                for t in range(TG):
                    last = nc.tensor.matmul(route_ps[:, TABLE:TABLE + 2 * SG], ohB[:, t, :],
                                            rhsA[:, t, :, :].rearrange("p k a -> p (k a)"), start=(t == 0), stop=(t == TG - 1))
                last.then_inc(table_done, 1)

            def x_transpose(q):
                pe.wait_ge(xg_done[q % 2], 32 * (q // 2 + 1))
                if q >= 2:
                    pe.wait_ge(xgT_done, q - 1)
                for j in range(2):
                    last = nc.tensor.transpose(xT_ps[q % 2][:, j * P:(j + 1) * P], xg[:, 2 * q + j, :], ident)
                last.then_inc(xT_done, 1)

            def experts(q):
                g, a = q // QG, 2 * (q % QG)
                if q % QG == 0:
                    pe.wait_ge(texp_done, g + 1)
                return [pe.value_load(texp[0:1, g, a + j:a + j + 1], min_val=0, max_val=E - 1) for j in range(2)]

            def up(q, e):
                pe.wait_ge(xgT_done, q + 1)
                if q == 0:
                    pe.wait_ge(ld_w1, 16)
                    pe.wait_ge(bias_ready, 16)
                if q >= 2:
                    pe.wait_ge(gelu_done, q - 1)
                for j in range(2):
                    o = h_ps[q % 2][:, j * H:(j + 1) * H]
                    nc.tensor.matmul(o, xgT[:, q % 2, j * P:(j + 1) * P], w1[:, bass.ds(e[j] * H, H)], start=True, stop=False)
                    last = nc.tensor.matmul(o, cb[0:3, CB_ONES:CB_ONES + P], bias3[0:3, bass.ds(e[j] * H, H)], start=False, stop=True)
                last.then_inc(up_done, 1)

            def h_transpose(q):
                pe.wait_ge(gelu_done, q + 1)
                if q >= 2:
                    pe.wait_ge(hgT_done, q - 1)
                for j in range(2 * H // P):
                    last = nc.tensor.transpose(hT_ps[q % 2][:, j * P:(j + 1) * P], hg[:, q % 2, j * P:(j + 1) * P], ident)
                last.then_inc(hT_done, 1)

            w2f = w2[:, :, :, :].rearrange("p e k c -> p (e k c)")

            def down(q, e):
                pe.wait_ge(hgT_done, q + 1)
                if q == 0:
                    pe.wait_ge(ld_w2, 16)
                if q >= 2:
                    pe.wait_ge(o_done, q - 1)
                for j in range(2):
                    o = o_ps[q % 2][:, j * C:(j + 1) * C]
                    for k in range(H // P):
                        nc.tensor.matmul(o, hgT[:, q % 2, j, k, :], w2f[:, bass.ds(e[j] * H + k * C, C)], start=(k == 0), stop=False)
                    last = nc.tensor.matmul(o, cb[0:3, CB_ONES:CB_ONES + P], bias3[0:3, bass.ds(e[j] * C + E * H, C)],
                                            start=False, stop=True)
                last.then_inc(down_done, 1)

            gates(0)
            gates(1)
            router_weights()
            for s in range(2, B):
                gates(s)
                if s == BG + LAG:
                    rank(0)
                if s == BG + LAG + 1:
                    table(0)
                tokens(s - LAG)
            for s in range(B - LAG, B):
                tokens(s)
            x_transpose(0)
            x_transpose(1)
            e_now = experts(0)
            up(0, e_now)
            rank(1)
            table(1)
            for q in range(1, Q + 1):
                e_last = e_now
                h_transpose(q - 1)
                if q + 1 < Q:
                    x_transpose(q + 1)
                if q < Q:
                    e_now = experts(q)
                    up(q, e_now)
                down(q - 1, e_last)

        @block.scalar
        def _(act):
            def sigmoids(s):
                if s == 0:
                    act.wait_ge(gbias_ready, 2)
                if s >= 2:
                    act.wait_ge(h_done, s - 1)
                act.wait_ge(pre_done, s + 1)
                nc.scalar.activation(sg[:, s % 2, :], pre_ps[s % 2][:, :], ACT.Sigmoid, bias=gate_bias[:, 1:2]).then_inc(sg_done, 1)
                nc.scalar.activation(z[:, s % 2, :], k_ps[s % 2][:, :], ACT.Sigmoid, bias=gate_bias[:, 0:1])
                nc.scalar.activation(keep[:, s % 2, :], k_ps[s % 2][:, :], ACT.Sigmoid, bias=gate_bias[:, 2:3], scale=-1.0).then_inc(z_done, 1)

            def normalize(s):
                act.wait_ge(rstd_done, s + 1)
                for j in range(TB):
                    t = s * TB + j
                    last = nc.scalar.activation(x1[:, t, :], s_ps[s % 2][:, j * P:(j + 1) * P], ACT.Identity,
                                                bias=nmr[:, t:t + 1], scale=rstd[:, t:t + 1])
                last.then_inc(x1_done, 1)

            def score_sigmoids(g):
                act.wait_ge(sgap_done, g + 1)
                nc.scalar.activation(sp_[:, :, :], sgap[:, :, :], ACT.Sigmoid)
                nc.scalar.activation(sn_[:, :, :], sgap[:, :, :], ACT.Sigmoid, scale=-1.0).then_inc(sig_done, 1)

            def copy_xT(q):
                act.wait_ge(xT_done, q + 1)
                if q >= 2:
                    act.wait_ge(up_done, q - 1)
                nc.scalar.copy(xgT[:, q % 2, :], xT_ps[q % 2][:, 0:2 * P]).then_inc(xgT_done, 1)

            def gelu(q):
                act.wait_ge(up_done, q + 1)
                if q >= 2:
                    act.wait_ge(hT_done, q - 1)
                nc.scalar.activation(hg[:, q % 2, :], h_ps[q % 2][:, :], ACT.Gelu).then_inc(gelu_done, 1)

            for s in range(B + LAG):
                if s < B:
                    sigmoids(s)
                if s >= LAG:
                    normalize(s - LAG)
                if s - LAG == BG:
                    score_sigmoids(0)
            copy_xT(0)
            copy_xT(1)
            score_sigmoids(1)
            for q in range(Q):
                gelu(q)
                if q + 2 < Q:
                    copy_xT(q + 2)

        @block.gpsimd
        def _(pool):
            nc.gpsimd.memset(half[:, 0:TG], -0.5).then_inc(half_ready, 1)
            nc.gpsimd.memset(half[:, TG:2 * TG], 0.5).then_inc(half_ready, 1)
            pool.wait_ge(half_ready, 2)
            pool.wait_ge(rt_dve, 2)
            nc.gpsimd.tensor_tensor(rtmp[:, 2 * E:3 * E], rtmp[:, E:2 * E], half[0:R, TG:TG + E], ALU.pow).then_inc(rt_pool, 1)

            def add_input(s):
                pool.wait_ge(h_done, s + 1)
                if s >= RING4:
                    pool.wait_ge(logit_done, s - RING4 + 1)
                nc.gpsimd.tensor_tensor(sT[:, s % RING4, :], h[:, s % RING4, :], xT[:, tok(s)], ALU.add).then_inc(s_done, 1)

            def inverse_deviation(s):
                ts = tiles(s)
                pool.wait_ge(mv_done, s + 1)
                nc.gpsimd.tensor_scalar(nmean[:, ts], mv[:, ts, 0], -1.0, None, ALU.mult)
                nc.gpsimd.tensor_scalar(var1[:, ts], mv[:, ts, 1], LN_EPS, None, ALU.add).then_inc(pool_ln, 1)
                pool.wait_ge(pool_ln, 2 * s + 1)
                nc.gpsimd.tensor_tensor(rstd[:, ts], var1[:, ts], half[:, 0:TB], ALU.pow).then_inc(pool_ln, 1)
                pool.wait_ge(pool_ln, 2 * s + 2)
                nc.gpsimd.tensor_tensor(nmr[:, ts], nmean[:, ts], rstd[:, ts], ALU.mult).then_inc(rstd_done, 1)

            def gather_tokens(i):
                g, a = i // SG, i % SG
                q = i // 2
                if a == 0:
                    pool.wait_ge(gidx_done, g + 1)
                    pool.wait_ge(x1_stored[g], 16 * BG)
                if i % 2 == 0 and q >= 2:
                    pool.wait_ge(xg_done[q % 2], 32 * (q // 2))
                nc.gpsimd.indirect_dma_start(out=xg[:, i, :], out_offset=None, in_=x1_dram[g],
                                             in_offset=bass.IndirectOffsetOnAxis(ap=gidx[:, g, a:a + 1], axis=0)).then_inc(xg_done[q % 2], 16)

            def gather_outputs(i):
                g, t = i // TG, i % TG
                if t == 0:
                    pool.wait_ge(o_stored[g], 16 * QG)
                if i >= 4:
                    pool.wait_ge(og_done[i % 4], 16 * (i // 4))
                nc.gpsimd.indirect_dma_start(out=og[:, i, :], out_offset=None, in_=o_dram[g],
                                             in_offset=bass.IndirectOffsetOnAxis(ap=slot[:, g, t:t + 1], axis=0)).then_inc(og_done[i % 4], 16)

            def inverse_deviation2(s):
                ts = tiles(s)
                pool.wait_ge(mv2_done, s + 1)
                nc.gpsimd.tensor_scalar(var2[:, ts], mv2[:, ts, 1], LN_EPS, None, ALU.add).then_inc(pool_ln2, 1)
                pool.wait_ge(pool_ln2, s + 1)
                nc.gpsimd.tensor_tensor(rstd2[:, ts], var2[:, ts], half[:, 0:TB], ALU.pow).then_inc(rstd2_done, 1)

            n = 0
            for s in range(B + LAG):
                if s < B:
                    add_input(s)
                if s >= LAG:
                    inverse_deviation(s - LAG)
                if s >= BG + LAG:
                    for _ in range(2):
                        gather_tokens(n)
                        n += 1
            while n < 2 * Q:
                gather_tokens(n)
                n += 1
            for s in range(B):
                for j in range(TB):
                    gather_outputs(s * TB + j)
                if s:
                    inverse_deviation2(s - 1)
            inverse_deviation2(B - 1)

        @block.vector
        def _(dve):
            chain = [0]

            def link(ins, on):
                on[1] += 1
                ins.then_inc(on[0], 1)
                dve.wait_ge(on[0], on[1])

            dve.wait_ge(ld_gate, 64)
            nc.vector.tensor_scalar(gate_bias[:, 2:3], gate_bias[:, 0:1], -1.0, None, ALU.mult).then_inc(gbias_ready, 1)
            nc.vector.tensor_scalar(gate_bias[:, 3:4], gate_bias[:, 1:2], 0.5, None, ALU.add).then_inc(gbias_ready, 1)
            dve.wait_ge(gbias_ready, 2)

            def router_weights():
                nc.vector.memset(ones16[:, :], 1.0)
                dve.wait_ge(ld_rt, 32)
                nc.vector.tensor_tensor(rtmp[:, 0:E], wgT[:, :], wgT[:, :], ALU.mult).then_inc(rt_dve, 1)
                dve.wait_ge(rt_pe, 1)
                nc.vector.tensor_copy(rtmp[:, E:2 * E], route_ps[0:R, 0:E]).then_inc(rt_dve, 1)
                dve.wait_ge(rt_pool, 1)
                nc.vector.tensor_scalar(rtmp[:, 4 * E:5 * E], rtmp[:, 2 * E:3 * E], NORM_MIN, None, ALU.max).then_inc(rt_dve, 1)
                dve.wait_ge(rt_dve, 3)
                nc.vector.reciprocal(rtmp[:, 5 * E:6 * E], rtmp[:, 4 * E:5 * E]).then_inc(rt_dve, 1)
                dve.wait_ge(rt_dve, 4)
                nc.vector.tensor_tensor(rtmp[:, 3 * E:4 * E], wgT[:, :], rtmp[:, 5 * E:6 * E], ALU.mult).then_inc(rt_dve, 1)
                nc.vector.reduce_sum(rtmp[:, 0:1], wredT[:, :], AX.X).then_inc(rt_dve, 1)
                dve.wait_ge(rt_dve, 6)
                nc.vector.tensor_scalar(rtmp[:, 1:2], rtmp[:, 0:1], 1.0 / C, None, ALU.mult).then_inc(rc, 1)
                chain_rc[1] += 1
                dve.wait_ge(rc, chain_rc[1])
                nc.vector.tensor_scalar(wredc[:, :], wredT[:, :], rtmp[:, 1:2], None, ALU.subtract).then_inc(rt_dve, 1)
                dve.wait_ge(rt_pe, 2)
                nc.vector.tensor_copy(router[:, :], route_ps[:, 0:E]).then_inc(router_ready, 1)

            def split_biases():
                dve.wait_ge(ld_b, 32)
                nc.vector.tensor_copy(bpart[:, 0, :], braw[:, :]).then_inc(bsplit, 1)
                dve.wait_ge(bsplit, 1)
                nc.vector.tensor_tensor(brem[:, 0, :], braw[:, :], bpart[:, 0, :], ALU.subtract).then_inc(bsplit, 1)
                dve.wait_ge(bsplit, 2)
                nc.vector.tensor_copy(bpart[:, 1, :], brem[:, 0, :]).then_inc(bsplit, 1)
                dve.wait_ge(bsplit, 3)
                nc.vector.tensor_tensor(brem[:, 1, :], brem[:, 0, :], bpart[:, 1, :], ALU.subtract).then_inc(bsplit, 1)
                dve.wait_ge(bsplit, 4)
                nc.vector.tensor_copy(bpart[:, 2, :], brem[:, 1, :]).then_inc(bsplit, 1)

            chain_rc = [rc, 0]

            def candidate(s):
                dve.wait_ge(sg_done, s + 1)
                nc.vector.scalar_tensor_tensor(out=cand[:, s % 2, :], in0=pre_ps[s % 2][:, :], scalar=gate_bias[:, 3:4],
                                               in1=sg[:, s % 2, :], op0=ALU.add, op1=ALU.max).then_inc(cand_done, 1)

            def gated(s):
                dve.wait_ge(z_done, s + 1)
                dve.wait_ge(cand_done, s + 1)
                nc.vector.tensor_tensor(zcand[:, s % 2, :], z[:, s % 2, :], cand[:, s % 2, :], ALU.mult).then_inc(zcand_done, 1)

            def scan(s):
                dve.wait_ge(zcand_done, s + 1)
                if s >= RING4:
                    dve.wait_ge(s_done, s - RING4 + 1)
                nc.vector.tensor_tensor_scan(h[:, s % RING4, :], keep[:, s % 2, :], zcand[:, s % 2, :], 0.5,
                                             ALU.mult, ALU.add).then_inc(h_done, 1)

            def stats(s):
                dve.wait_ge(stok_done, s + 1)
                for j in range(TB):
                    last = nc.vector.bn_stats(st1[:, s % 2, j, :], s_ps[s % 2][:, j * P:(j + 1) * P])
                last.then_inc(st_done, 1)

            def mean_var(s):
                dve.wait_ge(st_done, s + 1)
                for j in range(TB):
                    last = nc.vector.bn_aggr(mv[:, s * TB + j, :], st1[:, s % 2, j, :])
                last.then_inc(mv_done, 1)

            def tile_cols(c, n, w):
                return cf[:, c:c + n * w].rearrange("p (t a) -> p t a", a=w)

            def over(ap, n):
                return ap.unsqueeze(2).to_broadcast([P, ap.shape[1], n])

            def route_experts(g):
                ch = chain_rc
                dve.wait_ge(logit_done, BG * (g + 1))
                L = logit_ps[:, 0:TG * E].rearrange("p (t e) -> p t e", e=E)
                link(nc.vector.reduce_max(mx[:, :], L, AX.X), ch)
                nc.vector.tensor_tensor(gap[:, g, :, :], L, over(mx[:, :], E), ALU.subtract).then_inc(gap_done, 1)
                dve.wait_ge(gap_done, g + 1)
                link(nc.vector.scalar_tensor_tensor(out=key[:, :, :], in0=gap[:, g, :, :], scalar=0.0,
                                                    in1=tile_cols(CF_DESC, TG, E), op0=ALU.is_equal, op1=ALU.mult), ch)
                link(nc.vector.reduce_max(kmx[:, :], key[:, :, :], AX.X), ch)
                link(nc.vector.tensor_tensor(oh[:, :, :].rearrange("p e t -> p t e"), key[:, :, :], over(kmx[:, :], E),
                                             ALU.is_equal), ch)
                nc.vector.tensor_tensor_scan(incl[:, :, :].rearrange("p e t -> p (e t)"), cf[:, CF_RESET:CF_RESET + E * TG],
                                             oh[:, :, :].rearrange("p e t -> p (e t)"), 0.0, ALU.mult, ALU.add).then_inc(incl_done, 1)

            def score_gap(g):
                dve.wait_ge(rstd_done, BG * (g + 1))
                nc.vector.tensor_tensor(sgap[:, :, :], gap[:, g, :, :], over(rstd[:, g * TG:(g + 1) * TG], E), ALU.mult).then_inc(sgap_done, 1)

            def route_slots(g):
                ch = chain_rc
                dve.wait_ge(rank_done, g + 1)
                link(nc.vector.tensor_scalar(cnt[:, 0, :], route_ps[:, COUNT:COUNT + E], float(P - 1), None, ALU.add), ch)
                link(nc.vector.tensor_scalar(cnt[:, 1, :], cnt[:, 0, :], 7, None, ALU.logical_shift_right), ch)
                link(nc.vector.tensor_tensor_scan(ends[:, :], cb[:, CB_ONES:CB_ONES + E], cnt[:, 1, :], 0.0, ALU.mult, ALU.add), ch)
                link(nc.vector.tensor_tensor(base[:, :], ends[:, :], cnt[:, 1, :], ALU.subtract), ch)
                link(nc.vector.scalar_tensor_tensor(out=posx[:, :, :], in0=over(base[:, :], TG), scalar=float(P),
                                                    in1=route_ps[:, RANK:RANK + E * TG].rearrange("p (e t) -> p e t", t=TG),
                                                    op0=ALU.mult, op1=ALU.add), ch)
                link(nc.vector.tensor_tensor(key[:, :, :].rearrange("p t e -> p (t e)").rearrange("p (e t) -> p e t", t=TG),
                                             posx[:, :, :], oh[:, :, :], ALU.mult), ch)
                with nc.allow_low_precision(reason="slots are whole numbers below 2**24"):
                    nc.vector.reduce_sum(slot[:, g, :], key[:, :, :].rearrange("p t e -> p (t e)").rearrange("p (e t) -> p t e", t=TG),
                                         AX.X).then_inc(slot_done, 1)
                dve.wait_ge(slot_done, g + 1)
                nc.vector.tensor_scalar(lane[:, 0, :], slot[:, g, :], P - 1, None, ALU.bitwise_and)
                link(nc.vector.tensor_scalar(lane[:, 1, :], slot[:, g, :], 7, None, ALU.logical_shift_right), ch)
                nc.vector.tensor_copy(lanef[:, :], lane[:, 0, :])
                link(nc.vector.tensor_tensor(ohA[:, :, :], tile_cols(CF_TILE, TG, SG), over(lane[:, 1, :], SG), ALU.is_equal), ch)
                nc.vector.tensor_tensor(rhsA[:, :, 0, :], ohA[:, :, :], tile_cols(CF_BASE, TG, SG), ALU.mult)
                nc.vector.tensor_scalar(rhsA[:, :, 1, :], ohA[:, :, :], cf[:, CF_PART:CF_PART + 1], None, ALU.mult)
                for t in range(TG):
                    last = nc.vector.tensor_scalar(ohB[:, t, :], cb[:, CB_SLOT:CB_SLOT + P], lanef[:, t:t + 1], None, ALU.is_equal)
                last.then_inc(table_ready, 1)
                link(nc.vector.tensor_tensor(tcmp[:, :, :], tile_cols(CF_TILE_E, SG, E),
                                             ends[:, :].unsqueeze(1).to_broadcast([P, SG, E]), ALU.is_ge), ch)
                link(nc.vector.reduce_sum(tsum[:, :], tcmp[:, :, :], AX.X), ch)
                nc.vector.tensor_scalar(texp[:, g, :], tsum[:, :], float(E - 1), None, ALU.min).then_inc(texp_done, 1)
                dve.wait_ge(table_done, g + 1)
                link(nc.vector.tensor_copy(tlow[:, :], route_ps[:, TABLE + SG:TABLE + 2 * SG]), ch)
                nc.vector.tensor_tensor(gidx[:, g, :], route_ps[:, TABLE:TABLE + SG], tlow[:, :], ALU.add).then_inc(gidx_done, 1)

            sch = [sc, 0]

            def scores(g):
                dve.wait_ge(sig_done, g + 1)
                link(nc.vector.reciprocal(rn_[:, :, :], sn_[:, :, :]), sch)
                link(nc.vector.tensor_tensor(rn_[:, :, :], rn_[:, :, :], sp_[:, :, :], ALU.mult), sch)
                link(nc.vector.reduce_sum(den[:, :], rn_[:, :, :], AX.X), sch)
                nc.vector.reciprocal(score[:, g, :], den[:, :]).then_inc(score_done, 1)

            def copy_hT(q):
                dve.wait_ge(hT_done, q + 1)
                if q >= 2:
                    dve.wait_ge(down_done, q - 1)
                nc.vector.tensor_copy(hgT[:, q % 2, :, :, :].rearrange("p j k n -> p (j k n)"), hT_ps[q % 2][:, :]).then_inc(hgT_done, 1)

            def copy_o(q):
                dve.wait_ge(down_done, q + 1)
                nc.vector.tensor_copy(osb[:, q, :], o_ps[q % 2][:, 0:2 * C]).then_inc(o_done, 1)

            def residual(s):
                g = s // BG
                if s % BG == 0:
                    dve.wait_ge(score_done, g + 1)
                    dve.wait_ge(x1_done, BG * (g + 1))
                for j in range(TB):
                    t = s * TB + j
                    dve.wait_ge(og_done[t % 4], 16 * (t // 4 + 1))
                    last = nc.vector.scalar_tensor_tensor(out=og[:, t, :], in0=og[:, t, :], scalar=score[:, g, t % TG:t % TG + 1],
                                                   in1=x1[:, t, :], op0=ALU.mult, op1=ALU.add)
                last.then_inc(res_done, 1)
                dve.wait_ge(res_done, s + 1)
                for j in range(TB):
                    last = nc.vector.bn_stats(st2[:, s * TB + j, :], og[:, s * TB + j, :])
                last.then_inc(st2_done, 1)
                dve.wait_ge(st2_done, s + 1)
                for j in range(TB):
                    last = nc.vector.bn_aggr(mv2[:, s * TB + j, :], st2[:, s * TB + j, :])
                last.then_inc(mv2_done, 1)

            def normalize2(s):
                dve.wait_ge(rstd2_done, s + 1)
                for j in range(TB):
                    t = s * TB + j
                    last = nc.vector.tensor_scalar(y[:, t, :], og[:, t, :], mv2[:, t, 0:1], rstd2[:, t:t + 1], ALU.subtract, ALU.mult)
                last.then_inc(y_done, 1)

            candidate(0)
            router_weights()
            gated(0)
            scan(0)
            for s in range(1, B + LAG):
                if s < B:
                    candidate(s)
                    if s >= LAG:
                        stats(s - LAG)
                    gated(s)
                    if s >= LAG:
                        mean_var(s - LAG)
                    scan(s)
                else:
                    stats(s - LAG)
                    mean_var(s - LAG)
                if s == 1:
                    split_biases()
                if s == BG + LAG - 1:
                    route_experts(0)
                    score_gap(0)
                    route_slots(0)
                if s == BG + LAG:
                    scores(0)
            route_experts(1)
            score_gap(1)
            route_slots(1)
            scores(1)
            for q in range(Q):
                copy_hT(q)
                copy_o(q)
                if q in COMBINE_AFTER:
                    s = COMBINE_AFTER.index(q)
                    residual(s)
                if q - 1 in COMBINE_AFTER:
                    normalize2(COMBINE_AFTER.index(q - 1))
            for s in range(BG, B):
                residual(s)
                if s > BG:
                    normalize2(s - 1)
            normalize2(B - 1)


def kernel(L0_attn_x, L0_attn_Wz, L0_attn_bz, L0_attn_Wh, L0_attn_bh, L0_ffn_w_red, L0_ffn_wg, L0_ffn_W1, L0_ffn_b1,
           L0_ffn_W2, L0_ffn_b2):
    import numpy as np
    import ml_dtypes
    import concourse.bacc as bacc
    from concourse import mybir as mb
    from concourse.bass_utils import run_bass_kernel_spmd

    cf = np.zeros((P, CF_END), np.float32)
    cf[:, CF_IDENT:CF_IDENT + P] = np.eye(P)
    cf[:, CF_DESC:CF_RESET] = np.tile(np.arange(E, 0, -1), TG)
    cf[:, CF_RESET:CF_TILE] = np.tile(np.arange(TG) > 0, E)
    cf[:, CF_TILE:CF_BASE] = np.tile(np.arange(SG), TG)
    cf[:, CF_BASE:CF_TILE_E] = np.repeat(P * np.arange(TG), SG)
    cf[:, CF_TILE_E:CF_PART] = np.repeat(np.arange(SG), E)
    cf[:, CF_PART] = np.arange(P)
    cb = np.zeros((P, CB_END), np.float32)
    cb[:, CB_BEFORE:CB_ONES] = np.where(np.arange(P)[:, None] < np.arange(P)[None, :], 0, -1)
    cb[:, CB_ONES:CB_SLOT] = 1
    cb[:, CB_SLOT:CB_END] = np.arange(P)
    arrays = {
        "xT": np.ascontiguousarray(np.asarray(L0_attn_x).reshape(N, C).T),
        "wzT": np.ascontiguousarray(np.asarray(L0_attn_Wz).T),
        "whT": np.ascontiguousarray(np.asarray(L0_attn_Wh).T),
        "bz": np.asarray(L0_attn_bz).reshape(C, 1),
        "bh": np.asarray(L0_attn_bh).reshape(C, 1),
        "wredT": np.ascontiguousarray(np.asarray(L0_ffn_w_red).T),
        "wgT": np.ascontiguousarray(np.asarray(L0_ffn_wg).T),
        "w1": np.asarray(L0_ffn_W1),
        "b1": np.asarray(L0_ffn_b1),
        "w2": np.asarray(L0_ffn_W2),
        "b2": np.asarray(L0_ffn_b2),
        "cf": cf,
        "cb": cb.astype(ml_dtypes.bfloat16),
    }
    nc = bacc.Bacc("TRN2", target_bir_lowering=False, num_devices=1)
    args = [nc.dram_tensor(f"{n}_dram", a.shape, mb.dt.from_np(a.dtype), kind="ExternalInput").ap() for n, a in arrays.items()]
    out = nc.dram_tensor("out_dram", (N, C), mb.dt.float32, kind="ExternalOutput").ap()
    build_mingru_top1_moe(nc, *args, out)
    r = run_bass_kernel_spmd(nc, [{f"{n}_dram": a for n, a in arrays.items()}], core_ids=[0])
    return r.results[0]["out_dram"].reshape(B, S, C)
```

```python
import concourse.bass as bass
from concourse import mybir
from contextlib import ExitStack

B, S, C = 8, 512, 128
E, H, R = 8, 256, 16
P = 128
N = B * S
TB = S // P
G = 2
BG = B // G
TG = BG * TB
NG = TG * P
SG = (NG + E * (P - 1)) // P
QG = -(-SG // 2)
Q = G * QG
LN_EPS = 1e-5
NORM_MIN = 1e-4

CF_IDENT = 0
CF_DESC = CF_IDENT + P
CF_RESET = CF_DESC + TG * E
CF_TILE_E = CF_RESET + TG * E
CF_PART = CF_TILE_E + SG * E
CF_EXPERT = CF_PART + 1
CF_END = CF_EXPERT + 1
GW_WZ, GW_WH, GW_BZ, GW_BH, GW_END = 0, C, 2 * C, 2 * C + 1, 2 * C + 2
RW_RED, RW_WG, RW_END = 0, C, C + E
CB_BEFORE = 0
CB_ONES = CB_BEFORE + P
CB_SLOT = CB_ONES + P
CB_TILE = CB_SLOT + P
CB_BASE = CB_TILE + TG * SG
CB_END = CB_BASE + TG * SG


def build_mingru_top1_moe(nc, xT_d, gate_w_d, router_w_d, w1_d, b1_d, w2_d, b2_d, cf_d, cb_d, out_d):
    f32, bf16, i32, u32 = mybir.dt.float32, mybir.dt.bfloat16, mybir.dt.int32, mybir.dt.uint32
    ALU = mybir.AluOpType
    ACT = mybir.ActivationFunctionType
    AX = mybir.AxisListType

    x1_dram = [nc.dram_tensor(f"x1_rows_{g}", (NG, C), f32).ap() for g in range(G)]
    o_dram = [nc.dram_tensor(f"expert_out_rows_{g}", (SG * P, C), f32).ap() for g in range(G)]
    bias_dram = nc.dram_tensor("bias_parts", (3, E * H + E * C), bf16).ap()

    ctx = ExitStack()
    with ctx:
        def sb(name, shape, dt=f32):
            return ctx.enter_context(nc.sbuf_tensor(name, shape, dt))

        def sem(name):
            return ctx.enter_context(nc.semaphore(name))

        RING, RING4 = 2, 4
        xT = sb("xT", [P, N])
        gate_w = sb("gate_w", [P, GW_END])
        wz, wh = gate_w[:, GW_WZ:GW_WZ + C], gate_w[:, GW_WH:GW_WH + C]
        bz, bh = gate_w[:, GW_BZ:GW_BZ + 1], gate_w[:, GW_BH:GW_BH + 1]
        gate_bias = sb("gate_bias", [P, 2])
        cf = sb("cf", [P, CF_END])
        cb = sb("cb", [P, CB_END], bf16)
        w1 = sb("w1", [P, E * H])
        w2 = sb("w2", [P, E, H // P, C])
        keep = sb("keep", [P, RING, S])
        z = sb("z", [P, RING, S])
        sg = sb("sg", [P, RING, S])
        cand = sb("cand", [P, RING, S])
        zcand = sb("zcand", [P, RING, S])
        h = sb("h", [P, RING4, S])
        sT = sb("sT", [P, RING4, S])
        st1 = sb("st1", [P, RING, TB, 6])
        mv = sb("mv", [P, B * TB, 2])
        var1 = sb("var1", [P, B * TB])
        rstd = sb("rstd", [P, B * TB])
        nmean = sb("nmean", [P, B * TB])
        nmr = sb("nmr", [P, B * TB])
        x1 = sb("x1", [P, B * TB, C])
        router_w = sb("router_w", [R, RW_END])
        wredT, wgT = router_w[:, RW_RED:RW_RED + C], router_w[:, RW_WG:RW_WG + E]
        wredc = sb("wredc", [R, C])
        wg_sq = sb("wg_sq", [R, E])
        red_mean = sb("red_mean", [R, 2])
        norm_sq = sb("norm_sq", [P, E])
        inv_norm = sb("inv_norm", [P, E])
        ones16 = sb("ones16", [R, P])
        half = sb("half", [P, TG])
        router = sb("router", [P, E])
        braw = sb("braw", [P, 24])
        brem = sb("brem", [P, 2, 24])
        bpart = sb("bpart", [P, 3, 24], bf16)
        bias = sb("bias", [3 * E, H + C], bf16)
        pick = sb("pick", [3 * E, G, SG], bf16)
        mx = sb("mx", [P, TG])
        gap = sb("gap", [P, G, TG, E])
        key = sb("key", [P, TG, E])
        kmx = sb("kmx", [P, TG])
        oh = sb("oh", [P, E, TG], bf16)
        incl = sb("incl", [P, E, TG], bf16)
        cnt = sb("cnt", [P, 2, E], i32)
        ends = sb("ends", [P, E])
        base = sb("base", [P, E])
        rsel = sb("rsel", [P, E, TG])
        bsel = sb("bsel", [P, E, TG])
        tok_rank = sb("tok_rank", [P, TG], u32)
        tok_base = sb("tok_base", [P, TG])
        slot = sb("slot", [P, G, TG], u32)
        lane = sb("lane", [P, TG], u32)
        lanef = sb("lanef", [P, TG])
        rtile = sb("rtile", [P, TG], u32)
        tile_of = sb("tile_of", [P, TG])
        ohB = sb("ohB", [P, TG, P], bf16)
        ohA = sb("ohA", [P, TG, SG], bf16)
        rhsA = sb("rhsA", [P, 2, TG, SG], bf16)
        gidx = sb("gidx", [P, G, SG], u32)
        tcmp = sb("tcmp", [P, SG, E])
        tsum = sb("tsum", [P, SG])
        texp = sb("texp", [P, G, SG], i32)
        sgap = sb("sgap", [P, TG, E])
        sp_ = sb("sp_", [P, TG, E])
        sn_ = sb("sn_", [P, TG, E])
        rn_ = sb("rn_", [P, TG, E])
        den = sb("den", [P, TG])
        score = sb("score", [P, G, TG])
        xg = sb("xg", [P, Q * 2, C])
        xgT = sb("xgT", [P, RING, 2 * P])
        w1x = sb("w1x", [P, RING4, 2, H])
        hgT = sb("hgT", [P, RING, 2, H // P, P])
        osb = sb("osb", [P, Q, 2 * C])
        og = sb("og", [P, B * TB, C])
        st2 = sb("st2", [P, B * TB, 6])
        mv2 = sb("mv2", [P, B * TB, 2])
        eps = sb("eps", [P, 1])
        dev2 = sb("dev2", [P, B * TB])
        rstd2 = sb("rstd2", [P, B * TB])
        y = og

        bank = [ctx.enter_context(nc.psum_tensor(f"bank{i}", [P, 512], f32)) for i in range(8)]
        k_ps, pre_ps, s_ps = bank[0:2], bank[2:4], bank[4:6]
        logit_ps, route_ps = bank[6], bank[7]
        xT_ps, hT_ps, o_ps = bank[0:2], bank[2:4], bank[4:6]
        RANK, COUNT, TABLE = 0, 128, 160

        ld_gate, ld_rt, ld_cf, ld_cb, ld_w1, ld_w2, ld_b = (sem(n) for n in (
            "gate_weights_loaded", "router_weights_loaded", "constants_loaded", "bf16_constants_loaded",
            "w1_loaded", "w2_loaded", "biases_loaded"))
        ld_x = [sem(f"x_loaded_{s}") for s in range(B)]
        gbias_ready = sem("gate_bias_ready")
        half_ready = sem("half_ready")
        rt_dve, rt_pe = sem("router_dve"), sem("router_pe")
        norm_ready, inv_norm_ready = sem("router_norms_ready"), sem("router_inverse_norms_ready")
        router_ready = sem("router_ready")
        bsplit, bstored, bias_ready = sem("bias_split"), sem("bias_stored"), sem("bias_loaded")
        k_done, pre_done = sem("k_done"), sem("pre_done")
        z_done, keep_done, sg_done = sem("z_done"), sem("keep_done"), sem("sg_done")
        cand_done, zcand_done, h_done = sem("cand_done"), sem("zcand_done"), sem("h_done")
        s_done, stok_done, logit_done = sem("s_done"), sem("s_tokens_done"), sem("logits_done")
        st_done, mv_done = sem("stats_done"), sem("mean_var_done")
        pool_ln, rstd_done, x1_done = sem("pool_ln_chain"), sem("rstd_done"), sem("x1_done")
        s_read, var_ready, rstd_late = sem("s_tokens_read"), sem("late_var_ready"), sem("late_rstd_ready")
        x1_stored = [sem(f"x1_stored_{g}") for g in range(G)]
        gap_done = sem("gap_done")
        rc = sem("route_chain")
        rk, bs, rhs_ready, lane_ready, pool_lanes = (sem(n) for n in (
            "rank_chain", "base_chain", "table_rhs_ready", "lane_ready", "pool_lanes_ready"))
        incl_done, rank_done, table_ready, table_done = sem("incl_done"), sem("rank_done"), sem("table_ready"), sem("table_done")
        gidx_done, texp_done = sem("gather_index_done"), sem("tile_expert_done")
        slot_done = sem("slot_done")
        sgap_done, sig_done, score_done = sem("score_gap_done"), sem("score_sigmoids_done"), sem("score_done")
        sc = sem("score_chain")
        xg_done = [sem(f"x_gathered_{i}") for i in range(4)]
        xT_done, xgT_done, up_done, gelu_done = sem("x_transposed"), sem("xgT_copied"), sem("up_done"), sem("gelu_done")
        w1x_done, down_done, o_done = sem("w1_of_tiles_copied"), sem("down_done"), sem("o_copied")
        o_stored = [sem(f"o_stored_{g}") for g in range(G)]
        og_done = [sem(f"o_gathered_{i}") for i in range(4)]
        res_done, st2_done, mv2_done, rstd2_done = sem("residual_done"), sem("stats2_done"), sem("mean_var2_done"), sem("rstd2_done")
        eps_ready, dev2_done = sem("eps_ready"), sem("deviations2_done")
        y_done, out_stored = sem("y_done"), sem("out_stored")

        LAG = 2
        pair_tiles = lambda q: 2 if 2 * (q % QG) + 1 < SG else 1
        first_tile = lambda q: (q // QG) * SG + 2 * (q % QG)
        tok = lambda s: slice(s * S, (s + 1) * S)
        tiles = lambda s: slice(s * TB, (s + 1) * TB)

        landed = lambda q: sum(16 * pair_tiles(i) for i in range(q % 4, q + 1, 4))
        POOL_TILES = lambda g: 4 if g == 0 else 0
        TABLE_AFTER = 3
        LATE_LN_AFTER = 7
        table_base = lambda g: g * (TG - POOL_TILES(0))

        block = ctx.enter_context(nc.Block())

        @block.sync
        def _(sp):
            sp.dma_start(gate_w[:, :], gate_w_d).then_inc(ld_gate, 16)
            sp.dma_start(xT[:, tok(0)], xT_d[:, tok(0)]).then_inc(ld_x[0], 16)
            sp.dma_start(router_w[:, :], router_w_d).then_inc(ld_rt, 16)
            for s in range(1, B):
                sp.dma_start(xT[:, tok(s)], xT_d[:, tok(s)]).then_inc(ld_x[s], 16)
                if s == 1:
                    sp.dma_start(cf[:, :], cf_d).then_inc(ld_cf, 16)
                if s == 3:
                    sp.dma_start(cb[:, :], cb_d).then_inc(ld_cb, 16)
            sp.dma_start(braw[:, 0:16], b1_d.rearrange("e h -> (e h)").rearrange("(p f) -> p f", p=P)).then_inc(ld_b, 16)
            sp.dma_start(braw[:, 16:24], b2_d.rearrange("e h -> (e h)").rearrange("(p f) -> p f", p=P)).then_inc(ld_b, 16)
            sp.dma_start(w1[:, :].rearrange("c (e h) -> c e h", e=E), w1_d.rearrange("e c h -> c e h")).then_inc(ld_w1, 16)
            sp.dma_start(w2[:, :, :, :], w2_d.rearrange("e (k p) c -> p e k c", p=P)).then_inc(ld_w2, 16)
            sp.wait_ge(bsplit, 5)
            sp.dma_start(bias_dram[:, 0:E * H].rearrange("k (p f) -> p k f", p=P), bpart[:, :, 0:16]).then_inc(bstored, 16)
            sp.dma_start(bias_dram[:, E * H:].rearrange("k (p f) -> p k f", p=P), bpart[:, :, 16:24]).then_inc(bstored, 16)
            sp.wait_ge(bstored, 32)
            for k in range(3):
                sp.dma_start(bias[k:3 * E:3, 0:H], bias_dram[k, 0:E * H].rearrange("(e h) -> e h", e=E)).then_inc(bias_ready, 16)
                sp.dma_start(bias[k:3 * E:3, H:], bias_dram[k, E * H:].rearrange("(e c) -> e c", e=E)).then_inc(bias_ready, 16)
            for s in range(B):
                g, t0 = s // BG, (s % BG) * TB
                if s < BG:
                    sp.wait_ge(s_read, s + 1)
                else:
                    sp.wait_ge(x1_done, s - BG + 1)
                sp.dma_start(x1_dram[g][t0 * P:(t0 + TB) * P, :].rearrange("(t p) c -> p t c", p=P),
                             x1[:, tiles(s), :]).then_inc(x1_stored[g], 16)

            def store_pair(q):
                g, a = q // QG, 2 * (q % QG)
                sp.wait_ge(o_done, q + 1)
                n = pair_tiles(q)
                sp.dma_start(o_dram[g][a * P:(a + n) * P, :].rearrange("(t p) c -> p t c", p=P),
                             osb[:, q, 0:n * C].rearrange("p (t c) -> p t c", t=n)).then_inc(o_stored[g], 16)

            def store_out(t, n):
                sp.wait_ge(y_done, t + n)
                sp.dma_start(out_d[t * P:(t + n) * P, :].rearrange("(t p) c -> p t c", p=P), y[:, t:t + n, :]).then_inc(out_stored, 16)

            for q in range(Q):
                store_pair(q)
            for t in range(0, B * TB - TB, TB):
                store_out(t, TB)
            store_out(B * TB - TB, TB // 2)
            store_out(B * TB - TB // 2, TB // 2)
            sp.wait_ge(out_stored, 16 * (B + 1))

        @block.tensor
        def _(pe):
            ident = cf[:, CF_IDENT:CF_IDENT + P]

            def gates(s):
                if s == 0:
                    pe.wait_ge(ld_gate, 16)
                pe.wait_ge(ld_x[s], 16)
                if s >= 2:
                    pe.wait_ge(z_done, s - 1)
                    pe.wait_ge(cand_done, s - 1)
                nc.tensor.matmul(pre_ps[s % 2][:, :], wh, xT[:, tok(s)], start=True, stop=True).then_inc(pre_done, 1)
                nc.tensor.matmul(k_ps[s % 2][:, :], wz, xT[:, tok(s)], start=True, stop=True).then_inc(k_done, 1)

            def router_weights():
                pe.wait_ge(rt_dve, 4)
                nc.tensor.matmul(route_ps[:, 0:E], ones16[:, :], wg_sq[:, :], start=True, stop=True)
                nc.tensor.matmul(route_ps[:, E:2 * E], wredc[:, :], wgT, start=True, stop=True).then_inc(rt_pe, 1)

            def to_tokens(s):
                if s >= 2:
                    pe.wait_ge(s_read, s - 1)
                for j in range(TB):
                    last = nc.tensor.transpose(s_ps[s % 2][:, j * P:(j + 1) * P], sT[:, s % RING4, j * P:(j + 1) * P], ident)
                last.then_inc(stok_done, 1)

            def logits(s):
                if s == 0:
                    pe.wait_ge(router_ready, 1)
                if s % BG == 0 and s:
                    pe.wait_ge(gap_done, s // BG)
                for j in range(TB):
                    t = (s % BG) * TB + j
                    last = nc.tensor.matmul(logit_ps[:, t * E:(t + 1) * E], sT[:, s % RING4, j * P:(j + 1) * P],
                                            router[:, :], start=True, stop=True)
                last.then_inc(logit_done, 1)

            def tokens(s):
                pe.wait_ge(s_done, s + 1)
                if s == 0:
                    pe.wait_ge(ld_cf, 16)
                if s % BG == BG - 1:
                    logits(s)
                    to_tokens(s)
                else:
                    to_tokens(s)
                    logits(s)

            def rank(g):
                pe.wait_ge(incl_done, g + 1)
                if g == 0:
                    pe.wait_ge(ld_cb, 16)
                if g:
                    pe.wait_ge(gidx_done, g)
                flat_oh = oh[:, :, :].rearrange("p e t -> p (e t)")
                flat_incl = incl[:, :, :].rearrange("p e t -> p (e t)")
                nc.tensor.matmul(route_ps[:, RANK:RANK + E * TG], cb[:, CB_BEFORE:CB_BEFORE + P], flat_oh, start=True, stop=False)
                nc.tensor.matmul(route_ps[:, RANK:RANK + E * TG], cb[:, CB_ONES:CB_ONES + P], flat_incl, start=False, stop=True)
                nc.tensor.matmul(route_ps[:, COUNT:COUNT + E], cb[:, CB_ONES:CB_ONES + P], incl[:, :, TG - 1],
                                 start=True, stop=True).then_inc(rank_done, 1)

            def table(g):
                pe.wait_ge(rhs_ready, 2 * (g + 1))
                for t in range(TG):
                    if t < TG - POOL_TILES(g):
                        pe.wait_ge(table_ready, table_base(g) + t + 1)
                    elif t == TG - POOL_TILES(g):
                        pe.wait_ge(pool_lanes, POOL_TILES(g))
                    for k in range(2):
                        last = nc.tensor.matmul(route_ps[:, TABLE:TABLE + SG], ohB[:, t, :], rhsA[:, k, t, :],
                                                start=(t == 0 and k == 0), stop=(t == TG - 1 and k == 1))
                last.then_inc(table_done, 1)

            def x_transpose(q):
                pe.wait_ge(xg_done[q % 4], landed(q))
                if q >= 2:
                    pe.wait_ge(xgT_done, q - 1)
                for j in range(pair_tiles(q)):
                    last = nc.tensor.transpose(xT_ps[q % 2][:, j * P:(j + 1) * P], xg[:, first_tile(q) + j, :], ident)
                last.then_inc(xT_done, 1)

            def experts(q):
                g, a = q // QG, 2 * (q % QG)
                if q % QG == 0:
                    pe.wait_ge(texp_done, g + 1)
                _, e = nc.values_load_multi_w_load_instructions(
                    texp[0:1, g, a:min(a + 4, SG)], engines=[mybir.EngineType.PE], min_val=0, max_val=E - 1,
                    skip_runtime_bounds_check_because="VectorE takes the minimum with E - 1 of a count that is never negative")
                return {q: e[0:2], q + 1: e[2:4]}

            def tile_pick(q, j):
                a = 2 * (q % QG) + j
                return pick[:, q // QG, a:a + 1].to_broadcast([3 * E, P])

            def up(q):
                pe.wait_ge(xgT_done, q + 1)
                pe.wait_ge(w1x_done, q + 1)
                if q == 0:
                    pe.wait_ge(bias_ready, 96)
                if q >= 2:
                    pe.wait_ge(gelu_done, q - 1)
                for j in range(pair_tiles(q)):
                    for k in range(H // P):
                        o = hT_ps[q % 2][:, (j * (H // P) + k) * P:(j * (H // P) + k + 1) * P]
                        nc.tensor.matmul(o, bias[:, k * P:(k + 1) * P], tile_pick(q, j), start=True, stop=False)
                        last = nc.tensor.matmul(o, w1x[:, q % RING4, j, k * P:(k + 1) * P], xgT[:, q % 2, j * P:(j + 1) * P],
                                                start=False, stop=True)
                last.then_inc(up_done, 1)

            w2f = w2[:, :, :, :].rearrange("p e k c -> p (e k c)")

            def down(q, e):
                pe.wait_ge(gelu_done, q + 1)
                if q == 0:
                    pe.wait_ge(ld_w2, 16)
                if q < 2:
                    pe.wait_ge(s_read, B - 1 + q)
                if q >= 2:
                    pe.wait_ge(o_done, q - 1)
                for j in range(pair_tiles(q)):
                    o = o_ps[q % 2][:, j * C:(j + 1) * C]
                    nc.tensor.matmul(o, tile_pick(q, j), bias[:, H:], start=True, stop=False)
                    for k in range(H // P):
                        last = nc.tensor.matmul(o, hgT[:, q % 2, j, k, :], w2f[:, bass.ds(e[j] * H + k * C, C)],
                                                start=False, stop=(k == H // P - 1))
                last.then_inc(down_done, 1)

            gates(0)
            router_weights()
            for s in range(1, B):
                if s == BG + 1:
                    tokens(BG - 1)
                    rank(0)
                gates(s)
                if s == BG + 1:
                    table(0)
                elif s >= LAG:
                    tokens(s - LAG)
            for s in range(B - LAG, B):
                tokens(s)
            x_transpose(0)
            x_transpose(1)
            up(0)
            rank(1)
            for q in range(Q):
                if q + 2 < Q:
                    x_transpose(q + 2)
                if q + 1 < Q:
                    up(q + 1)
                if q % 2 == 0:
                    e_of = experts(q)
                down(q, e_of[q])
                if q == TABLE_AFTER:
                    table(1)

        @block.scalar
        def _(act):
            def sigmoids(s):
                if s == 0:
                    act.wait_ge(gbias_ready, 2)
                if s >= 2:
                    act.wait_ge(h_done, s - 1)
                act.wait_ge(pre_done, s + 1)
                nc.scalar.activation(sg[:, s % 2, :], pre_ps[s % 2][:, :], ACT.Sigmoid, bias=bh).then_inc(sg_done, 1)
                act.wait_ge(k_done, s + 1)
                nc.scalar.activation(z[:, s % 2, :], k_ps[s % 2][:, :], ACT.Sigmoid, bias=bz)
                nc.scalar.activation(keep[:, s % 2, :], k_ps[s % 2][:, :], ACT.Sigmoid, bias=gate_bias[:, 0:1], scale=-1.0).then_inc(z_done, 1)

            def normalize(s):
                act.wait_ge(rstd_done, s + 1)
                for j in range(TB):
                    t = s * TB + j
                    last = nc.scalar.activation(x1[:, t, :], s_ps[s % 2][:, j * P:(j + 1) * P], ACT.Identity,
                                                bias=nmr[:, t:t + 1], scale=rstd[:, t:t + 1])
                last.then_inc(s_read, 1)

            def keep_tokens(s):
                act.wait_ge(st_done, s + 1)
                nc.scalar.copy(x1[:, tiles(s), :].rearrange("p t c -> p (t c)"), s_ps[s % 2][:, :]).then_inc(s_read, 1)

            def score_sigmoids(g):
                act.wait_ge(sgap_done, g + 1)
                nc.scalar.activation(sp_[:, :, :], sgap[:, :, :], ACT.Sigmoid)
                nc.scalar.activation(sn_[:, :, :], sgap[:, :, :], ACT.Sigmoid, scale=-1.0).then_inc(sig_done, 1)

            def deviations(s):
                ts = slice(0, TG) if s < BG else tiles(s)
                act.wait_ge(eps_ready, 1)
                act.wait_ge(mv2_done, ts.stop)
                nc.scalar.activation(dev2[:, ts], mv2[:, ts, 1], ACT.Sqrt, bias=eps[:, 0:1]).then_inc(dev2_done, 1)

            def copy_xT(q):
                act.wait_ge(xT_done, q + 1)
                if q >= 2:
                    act.wait_ge(up_done, q - 1)
                nc.scalar.copy(xgT[:, q % 2, 0:pair_tiles(q) * P], xT_ps[q % 2][:, 0:pair_tiles(q) * P]).then_inc(xgT_done, 1)

            def experts(q):
                g, a = q // QG, 2 * (q % QG)
                if q % QG == 0:
                    act.wait_ge(texp_done, g + 1)
                _, e = nc.values_load_multi_w_load_instructions(
                    texp[0:1, g, a:min(a + 4, SG)], engines=[mybir.EngineType.Activation], min_val=0, max_val=E - 1,
                    skip_runtime_bounds_check_because="VectorE takes the minimum with E - 1 of a count that is never negative")
                return {q: e[0:2], q + 1: e[2:4]}

            def copy_w1(q, e):
                if q == 0:
                    act.wait_ge(ld_w1, 16)
                if q >= RING4:
                    act.wait_ge(up_done, q - RING4 + 1)
                for j in range(pair_tiles(q)):
                    last = nc.scalar.copy(w1x[:, q % RING4, j, :], w1[:, bass.ds(e[j] * H, H)])
                last.then_inc(w1x_done, 1)

            def gelu(q):
                act.wait_ge(up_done, q + 1)
                if q >= 2:
                    act.wait_ge(down_done, q - 1)
                nc.scalar.activation(hgT[:, q % 2, 0:pair_tiles(q), :, :].rearrange("p j k n -> p (j k n)"),
                                     hT_ps[q % 2][:, 0:pair_tiles(q) * H], ACT.Gelu).then_inc(gelu_done, 1)

            for s in range(B + LAG + 1):
                if s < B:
                    sigmoids(s)
                if LAG < s <= LAG + BG:
                    normalize(s - LAG - 1)
                elif s > LAG:
                    keep_tokens(s - LAG - 1)
                if s == B:
                    score_sigmoids(0)
            e_of = experts(0)
            for q in range(2):
                copy_w1(q, e_of[q])
                copy_xT(q)
            for q in range(Q):
                gelu(q)
                if q + 2 < Q:
                    copy_xT(q + 2)
                    if q % 2 == 0:
                        e_of = experts(q + 2)
                    copy_w1(q + 2, e_of[q + 2])
            score_sigmoids(1)
            for s in range(BG - 1, B):
                deviations(s)

        @block.gpsimd
        def _(pool):
            nc.gpsimd.memset(half[:, :], -0.5).then_inc(half_ready, 1)
            nc.gpsimd.memset(eps[:, :], LN_EPS).then_inc(eps_ready, 1)
            pool.wait_ge(half_ready, 1)
            pool.wait_ge(norm_ready, 1)
            nc.gpsimd.tensor_tensor(inv_norm[:, :], norm_sq[:, :], half[:, 0:E], ALU.pow).then_inc(inv_norm_ready, 1)

            def split_biases():
                pool.wait_ge(ld_b, 32)
                nc.gpsimd.tensor_copy(bpart[:, 0, :], braw[:, :]).then_inc(bsplit, 1)
                pool.wait_ge(bsplit, 1)
                nc.gpsimd.tensor_tensor(brem[:, 0, :], braw[:, :], bpart[:, 0, :], ALU.subtract).then_inc(bsplit, 1)
                pool.wait_ge(bsplit, 2)
                nc.gpsimd.tensor_copy(bpart[:, 1, :], brem[:, 0, :]).then_inc(bsplit, 1)
                pool.wait_ge(bsplit, 3)
                nc.gpsimd.tensor_tensor(brem[:, 1, :], brem[:, 0, :], bpart[:, 1, :], ALU.subtract).then_inc(bsplit, 1)
                pool.wait_ge(bsplit, 4)
                nc.gpsimd.tensor_copy(bpart[:, 2, :], brem[:, 1, :]).then_inc(bsplit, 1)

            def add_input(s):
                pool.wait_ge(h_done, s + 1)
                if s >= RING4:
                    pool.wait_ge(logit_done, s - RING4 + 1)
                nc.gpsimd.tensor_tensor(sT[:, s % RING4, :], h[:, s % RING4, :], xT[:, tok(s)], ALU.add).then_inc(s_done, 1)

            def inverse_deviation(s):
                ts = tiles(s)
                pool.wait_ge(mv_done, s + 1)
                nc.gpsimd.tensor_scalar(nmean[:, ts], mv[:, ts, 0], -1.0, None, ALU.mult)
                nc.gpsimd.tensor_scalar(var1[:, ts], mv[:, ts, 1], LN_EPS, None, ALU.add).then_inc(pool_ln, 1)
                pool.wait_ge(pool_ln, 2 * s + 1)
                nc.gpsimd.tensor_tensor(rstd[:, ts], var1[:, ts], half[:, 0:TB], ALU.pow).then_inc(pool_ln, 1)
                pool.wait_ge(pool_ln, 2 * s + 2)
                nc.gpsimd.tensor_tensor(nmr[:, ts], nmean[:, ts], rstd[:, ts], ALU.mult).then_inc(rstd_done, 1)

            def gather_tokens(q):
                g = q // QG
                if q % QG == 0:
                    pool.wait_ge(gidx_done, g + 1)
                    pool.wait_ge(x1_stored[g], 16 * BG)
                if q >= 4:
                    pool.wait_ge(xg_done[q % 4], landed(q - 4))
                for j in range(pair_tiles(q)):
                    a = 2 * (q % QG) + j
                    nc.gpsimd.indirect_dma_start(out=xg[:, first_tile(q) + j, :], out_offset=None, in_=x1_dram[g],
                                                 in_offset=bass.IndirectOffsetOnAxis(ap=gidx[:, g, a:a + 1], axis=0)
                                                 ).then_inc(xg_done[q % 4], 16)

            def gather_outputs(i):
                g, t = i // TG, i % TG
                if t == 0:
                    pool.wait_ge(o_stored[g], 16 * QG)
                if i >= 4:
                    pool.wait_ge(og_done[i % 4], 16 * (i // 4))
                nc.gpsimd.indirect_dma_start(out=og[:, i, :], out_offset=None, in_=o_dram[g],
                                             in_offset=bass.IndirectOffsetOnAxis(ap=slot[:, g, t:t + 1], axis=0)).then_inc(og_done[i % 4], 16)

            def late_inverse_deviations():
                pool.wait_ge(var_ready, 1)
                nc.gpsimd.tensor_tensor(rstd[:, TG:2 * TG], var1[:, TG:2 * TG], half[:, :], ALU.pow).then_inc(rstd_late, 1)

            def table_lanes(g):
                pool.wait_ge(ld_cb, 16)
                pool.wait_ge(lane_ready, g + 1)
                for t in range(TG - POOL_TILES(g), TG):
                    nc.gpsimd.tensor_scalar(ohB[:, t, :], cb[:, CB_SLOT:CB_SLOT + P], lanef[:, t:t + 1], None,
                                            ALU.is_equal).then_inc(pool_lanes, 1)

            for s in range(BG + LAG):
                if s < BG - 1:
                    add_input(s)
                if s >= LAG:
                    inverse_deviation(s - LAG)
                if s == 2:
                    split_biases()
            table_lanes(0)
            for q in range(Q):
                gather_tokens(q)
                if q == LATE_LN_AFTER:
                    late_inverse_deviations()
            for i in range(B * TB):
                gather_outputs(i)

        @block.vector
        def _(dve):
            chain = [0]

            def link(ins, on):
                on[1] += 1
                ins.then_inc(on[0], 1)
                dve.wait_ge(on[0], on[1])

            dve.wait_ge(ld_gate, 16)
            nc.vector.tensor_scalar(gate_bias[:, 0:1], bz, -1.0, None, ALU.mult).then_inc(gbias_ready, 1)
            nc.vector.tensor_scalar(gate_bias[:, 1:2], bh, 0.5, None, ALU.add).then_inc(gbias_ready, 1)
            dve.wait_ge(gbias_ready, 2)

            def router_weights():
                nc.vector.memset(ones16[:, :], 1.0).then_inc(rt_dve, 1)
                dve.wait_ge(ld_rt, 16)
                nc.vector.reduce_sum(red_mean[:, 0:1], wredT, AX.X).then_inc(rt_dve, 1)
                dve.wait_ge(rt_dve, 2)
                nc.vector.tensor_scalar(red_mean[:, 1:2], red_mean[:, 0:1], 1.0 / C, None, ALU.mult).then_inc(rt_dve, 1)
                nc.vector.tensor_tensor(wg_sq[:, :], wgT, wgT, ALU.mult)
                dve.wait_ge(rt_dve, 3)
                nc.vector.tensor_scalar(wredc[:, :], wredT, red_mean[:, 1:2], None, ALU.subtract).then_inc(rt_dve, 1)

            def router_norms():
                dve.wait_ge(rt_pe, 1)
                nc.vector.tensor_scalar(norm_sq[:, :], route_ps[:, 0:E], NORM_MIN * NORM_MIN, None, ALU.max).then_inc(norm_ready, 1)

            def scale_router():
                dve.wait_ge(inv_norm_ready, 1)
                nc.vector.tensor_tensor(router[:, :], route_ps[:, E:2 * E], inv_norm[:, :], ALU.mult).then_inc(router_ready, 1)

            chain_rc = [rc, 0]

            def candidate(s):
                dve.wait_ge(sg_done, s + 1)
                nc.vector.scalar_tensor_tensor(out=cand[:, s % 2, :], in0=pre_ps[s % 2][:, :], scalar=gate_bias[:, 1:2],
                                               in1=sg[:, s % 2, :], op0=ALU.add, op1=ALU.max).then_inc(cand_done, 1)

            def gated(s):
                dve.wait_ge(z_done, s + 1)
                dve.wait_ge(cand_done, s + 1)
                nc.vector.tensor_tensor(zcand[:, s % 2, :], z[:, s % 2, :], cand[:, s % 2, :], ALU.mult).then_inc(zcand_done, 1)

            def scan(s):
                dve.wait_ge(zcand_done, s + 1)
                if s >= RING4:
                    dve.wait_ge(s_done, s - RING4 + 1)
                nc.vector.tensor_tensor_scan(h[:, s % RING4, :], keep[:, s % 2, :], zcand[:, s % 2, :], 0.5,
                                             ALU.mult, ALU.add).then_inc(h_done, 1)

            def add_input(s):
                dve.wait_ge(h_done, s + 1)
                if s >= RING4:
                    dve.wait_ge(logit_done, s - RING4 + 1)
                nc.vector.tensor_tensor(sT[:, s % RING4, :], h[:, s % RING4, :], xT[:, tok(s)], ALU.add).then_inc(s_done, 1)

            def stats(s):
                dve.wait_ge(stok_done, s + 1)
                for j in range(TB):
                    last = nc.vector.bn_stats(st1[:, s % 2, j, :], s_ps[s % 2][:, j * P:(j + 1) * P])
                last.then_inc(st_done, 1)

            def mean_var(s):
                dve.wait_ge(st_done, s + 1)
                for j in range(TB):
                    last = nc.vector.bn_aggr(mv[:, s * TB + j, :], st1[:, s % 2, j, :])
                last.then_inc(mv_done, 1)

            def tile_cols(c, n, w):
                return cf[:, c:c + n * w].rearrange("p (t a) -> p t a", a=w)

            def over(ap, n):
                return ap.unsqueeze(2).to_broadcast([P, ap.shape[1], n])

            def route_experts(g):
                ch = chain_rc
                dve.wait_ge(logit_done, BG * (g + 1))
                L = logit_ps[:, 0:TG * E].rearrange("p (t e) -> p t e", e=E)
                link(nc.vector.reduce_max(mx[:, :], L, AX.X), ch)
                nc.vector.tensor_tensor(gap[:, g, :, :], L, over(mx[:, :], E), ALU.subtract).then_inc(gap_done, 1)
                dve.wait_ge(gap_done, g + 1)
                link(nc.vector.scalar_tensor_tensor(out=key[:, :, :], in0=gap[:, g, :, :], scalar=0.0,
                                                    in1=tile_cols(CF_DESC, TG, E), op0=ALU.is_equal, op1=ALU.mult), ch)
                link(nc.vector.reduce_max(kmx[:, :], key[:, :, :], AX.X), ch)
                link(nc.vector.tensor_tensor(oh[:, :, :].rearrange("p e t -> p t e"), key[:, :, :], over(kmx[:, :], E),
                                             ALU.is_equal), ch)
                nc.vector.tensor_tensor_scan(incl[:, :, :].rearrange("p e t -> p (e t)"), cf[:, CF_RESET:CF_RESET + E * TG],
                                             oh[:, :, :].rearrange("p e t -> p (e t)"), 0.0, ALU.mult, ALU.add).then_inc(incl_done, 1)

            def score_gap(g):
                if g == 0:
                    dve.wait_ge(rstd_done, BG)
                else:
                    dve.wait_ge(rstd_late, 1)
                nc.vector.tensor_tensor(sgap[:, :, :], gap[:, g, :, :], over(rstd[:, g * TG:(g + 1) * TG], E), ALU.mult).then_inc(sgap_done, 1)

            def by_expert(ap):
                return ap.rearrange("p e t -> p t e")

            def lanes(ts):
                for t in ts:
                    nc.vector.tensor_scalar(ohB[:, t, :], cb[:, CB_SLOT:CB_SLOT + P], lanef[:, t:t + 1], None,
                                            ALU.is_equal).then_inc(table_ready, 1)

            RK, BS = 3, 9

            def route_slots(g):
                dve.wait_ge(rank_done, g + 1)
                nc.vector.tensor_tensor(rsel[:, :, :], route_ps[:, RANK:RANK + E * TG].rearrange("p (e t) -> p e t", t=TG),
                                        oh[:, :, :], ALU.mult).then_inc(rk, 1)
                nc.vector.tensor_scalar(cnt[:, 0, :], route_ps[:, COUNT:COUNT + E], float(P - 1), None, ALU.add).then_inc(bs, 1)
                dve.wait_ge(rk, RK * g + 1)
                with nc.allow_low_precision(reason="ranks are whole numbers below 2**24"):
                    nc.vector.reduce_sum(tok_rank[:, :], by_expert(rsel[:, :, :]), AX.X).then_inc(rk, 1)
                dve.wait_ge(bs, BS * g + 1)
                nc.vector.tensor_scalar(cnt[:, 1, :], cnt[:, 0, :], 7, None, ALU.logical_shift_right).then_inc(bs, 1)
                dve.wait_ge(rk, RK * g + 2)
                nc.vector.tensor_scalar(lane[:, :], tok_rank[:, :], P - 1, None, ALU.bitwise_and).then_inc(rk, 1)
                dve.wait_ge(bs, BS * g + 2)
                nc.vector.tensor_tensor_scan(ends[:, :], cb[:, CB_ONES:CB_ONES + E], cnt[:, 1, :], 0.0, ALU.mult, ALU.add).then_inc(bs, 1)
                dve.wait_ge(rk, RK * g + 3)
                nc.vector.tensor_copy(lanef[:, :], lane[:, :]).then_inc(lane_ready, 1)
                dve.wait_ge(bs, BS * g + 3)
                nc.vector.tensor_tensor(base[:, :], ends[:, :], cnt[:, 1, :], ALU.subtract).then_inc(bs, 1)
                nc.vector.tensor_scalar(rtile[:, :], tok_rank[:, :], 7, None, ALU.logical_shift_right).then_inc(bs, 1)
                dve.wait_ge(bs, BS * g + 5)
                nc.vector.tensor_tensor(bsel[:, :, :], over(base[:, :], TG), oh[:, :, :], ALU.mult).then_inc(bs, 1)
                dve.wait_ge(lane_ready, g + 1)
                lanes(range(0, 1))
                dve.wait_ge(bs, BS * g + 6)
                nc.vector.reduce_sum(tok_base[:, :], by_expert(bsel[:, :, :]), AX.X).then_inc(bs, 1)
                lanes(range(1, 2))
                dve.wait_ge(bs, BS * g + 7)
                nc.vector.tensor_tensor(tile_of[:, :], tok_base[:, :], rtile[:, :], ALU.add).then_inc(bs, 1)
                lanes(range(2, 3))
                dve.wait_ge(bs, BS * g + 8)
                nc.vector.tensor_tensor(ohA[:, :, :], cb[:, CB_TILE:CB_TILE + TG * SG].rearrange("p (t a) -> p t a", a=SG),
                                        over(tile_of[:, :], SG), ALU.is_equal).then_inc(bs, 1)
                lanes(range(3, 4))
                dve.wait_ge(bs, BS * g + 9)
                nc.vector.tensor_tensor(rhsA[:, 0, :, :], ohA[:, :, :], cb[:, CB_BASE:CB_BASE + TG * SG].rearrange("p (t a) -> p t a", a=SG),
                                        ALU.mult).then_inc(rhs_ready, 1)
                nc.vector.tensor_scalar(rhsA[:, 1, :, :], ohA[:, :, :], cf[:, CF_PART:CF_PART + 1], None, ALU.mult).then_inc(rhs_ready, 1)

            def output_slots(g):
                nc.vector.scalar_tensor_tensor(out=slot[:, g, :], in0=tok_base[:, :], scalar=float(P), in1=tok_rank[:, :],
                                               op0=ALU.mult, op1=ALU.add).then_inc(slot_done, 1)

            def tile_experts(g):
                ch = chain_rc
                link(nc.vector.tensor_tensor(tcmp[:, :, :], tile_cols(CF_TILE_E, SG, E),
                                             ends[:, :].unsqueeze(1).to_broadcast([P, SG, E]), ALU.is_ge), ch)
                link(nc.vector.reduce_sum(tsum[:, :], tcmp[:, :, :], AX.X), ch)
                link(nc.vector.tensor_scalar(tsum[:, :], tsum[:, :], float(E - 1), None, ALU.min), ch)
                nc.vector.tensor_copy(texp[:, g, :], tsum[:, :])
                nc.vector.tensor_scalar(pick[:, g, :], tsum[0:3 * E, :], cf[0:3 * E, CF_EXPERT:CF_EXPERT + 1], None,
                                        ALU.is_equal).then_inc(texp_done, 1)

            def gather_index(g):
                dve.wait_ge(table_done, g + 1)
                nc.vector.tensor_copy(gidx[:, g, :], route_ps[:, TABLE:TABLE + SG]).then_inc(gidx_done, 1)

            sch = [sc, 0]

            def scores(g):
                dve.wait_ge(sig_done, g + 1)
                link(nc.vector.reciprocal(rn_[:, :, :], sn_[:, :, :]), sch)
                link(nc.vector.tensor_tensor(rn_[:, :, :], rn_[:, :, :], sp_[:, :, :], ALU.mult), sch)
                link(nc.vector.reduce_sum(den[:, :], rn_[:, :, :], AX.X), sch)
                nc.vector.reciprocal(score[:, g, :], den[:, :]).then_inc(score_done, 1)

            def copy_o(q):
                dve.wait_ge(down_done, q + 1)
                nc.vector.tensor_copy(osb[:, q, 0:pair_tiles(q) * C], o_ps[q % 2][:, 0:pair_tiles(q) * C]).then_inc(o_done, 1)

            def combine(i):
                if i < B * TB:
                    if i % TG == 0:
                        dve.wait_ge(score_done, i // TG + 1)
                        dve.wait_ge(s_read, BG)
                    dve.wait_ge(og_done[i % 4], 16 * (i // 4 + 1))
                    nc.vector.scalar_tensor_tensor(out=og[:, i, :], in0=og[:, i, :], scalar=score[:, i // TG, i % TG:i % TG + 1],
                                                   in1=x1[:, i, :], op0=ALU.mult, op1=ALU.add).then_inc(res_done, 1)
                if 1 <= i <= B * TB:
                    dve.wait_ge(res_done, i)
                    nc.vector.bn_stats(st2[:, i - 1, :], og[:, i - 1, :]).then_inc(st2_done, 1)
                if i >= 2:
                    dve.wait_ge(st2_done, i - 1)
                    nc.vector.bn_aggr(mv2[:, i - 2, :], st2[:, i - 2, :]).then_inc(mv2_done, 1)

            def normalize2(s):
                ts = slice(0, TG) if s < BG else tiles(s)
                n = s - BG + 2
                dve.wait_ge(dev2_done, n)
                nc.vector.reciprocal(rstd2[:, ts], dev2[:, ts]).then_inc(rstd2_done, 1)
                dve.wait_ge(rstd2_done, n)
                for t in range(ts.start, ts.stop):
                    nc.vector.tensor_scalar(y[:, t, :], og[:, t, :], mv2[:, t, 0:1], rstd2[:, t:t + 1],
                                            ALU.subtract, ALU.mult).then_inc(y_done, 1)

            def late_variances():
                dve.wait_ge(mv_done, B)
                nc.vector.tensor_scalar(var1[:, TG:2 * TG], mv[:, TG:2 * TG, 1], LN_EPS, None, ALU.add).then_inc(var_ready, 1)

            def normalize_late(s):
                dve.wait_ge(rstd_late, 1)
                dve.wait_ge(s_read, s + 1)
                for t in range(s * TB, (s + 1) * TB):
                    last = nc.vector.tensor_scalar(x1[:, t, :], x1[:, t, :], mv[:, t, 0:1], rstd[:, t:t + 1], ALU.subtract, ALU.mult)
                last.then_inc(x1_done, 1)

            router_weights()
            for s in range(B):
                candidate(s)
                if s == 0:
                    router_norms()
                if s >= LAG and s != BG + 1:
                    stats(s - LAG)
                if s == BG:
                    mean_var(s - LAG)
                    route_experts(0)
                    stats(BG - 1)
                    mean_var(BG - 1)
                    route_slots(0)
                    lanes(range(4, TG - POOL_TILES(0)))
                    tile_experts(0)
                    gated(s)
                    gather_index(0)
                    output_slots(0)
                else:
                    gated(s)
                    if s >= LAG and s != BG + 1:
                        mean_var(s - LAG)
                scan(s)
                if s >= BG - 1:
                    add_input(s)
                if s == 0:
                    scale_router()
            for s in range(B - LAG, B):
                stats(s)
                mean_var(s)
            late_variances()
            score_gap(0)
            route_experts(1)
            scores(0)
            for s in range(BG, B):
                normalize_late(s)
            score_gap(1)
            for q in range(Q):
                copy_o(q)
                if q == 0:
                    route_slots(1)
                if q == 1:
                    lanes(range(4, TG - 4))
                if q == 2:
                    lanes(range(TG - 4, TG))
                    tile_experts(1)
                    output_slots(1)
                if q == TABLE_AFTER:
                    gather_index(1)
            for i in range(B * TB + 2):
                if i == TG:
                    scores(1)
                combine(i)
                if i == TG + 3:
                    normalize2(BG - 1)
                if i > TG + TB + 1 and i % TB == 3:
                    normalize2(i // TB - 1)
            normalize2(B - 1)


def kernel(L0_attn_x, L0_attn_Wz, L0_attn_bz, L0_attn_Wh, L0_attn_bh, L0_ffn_w_red, L0_ffn_wg, L0_ffn_W1, L0_ffn_b1,
           L0_ffn_W2, L0_ffn_b2):
    import numpy as np
    import ml_dtypes
    import concourse.bacc as bacc
    from concourse import mybir as mb
    from concourse.bass_utils import run_bass_kernel_spmd

    cf = np.zeros((P, CF_END), np.float32)
    cf[:, CF_IDENT:CF_IDENT + P] = np.eye(P)
    cf[:, CF_DESC:CF_RESET] = np.tile(np.arange(E, 0, -1), TG)
    cf[:, CF_RESET:CF_TILE_E] = np.tile(np.arange(TG) > 0, E)
    cf[:, CF_TILE_E:CF_PART] = np.repeat(np.arange(SG), E)
    cf[:, CF_PART] = np.arange(P)
    cf[:, CF_EXPERT] = np.arange(P) // 3
    cb = np.zeros((P, CB_END), np.float32)
    cb[:, CB_BEFORE:CB_ONES] = np.where(np.arange(P)[:, None] < np.arange(P)[None, :], 0, -1)
    cb[:, CB_ONES:CB_SLOT] = 1
    cb[:, CB_SLOT:CB_TILE] = np.arange(P)
    cb[:, CB_TILE:CB_BASE] = np.tile(np.arange(SG), TG)
    cb[:, CB_BASE:CB_END] = np.repeat(P * np.arange(TG), SG)
    arrays = {
        "xT": np.ascontiguousarray(np.asarray(L0_attn_x).reshape(N, C).T),
        "gate_w": np.concatenate([np.asarray(L0_attn_Wz).T, np.asarray(L0_attn_Wh).T, np.asarray(L0_attn_bz).reshape(C, 1),
                                  np.asarray(L0_attn_bh).reshape(C, 1)], axis=1),
        "router_w": np.concatenate([np.asarray(L0_ffn_w_red).T, np.asarray(L0_ffn_wg).T], axis=1),
        "w1": np.asarray(L0_ffn_W1),
        "b1": np.asarray(L0_ffn_b1),
        "w2": np.asarray(L0_ffn_W2),
        "b2": np.asarray(L0_ffn_b2),
        "cf": cf,
        "cb": cb.astype(ml_dtypes.bfloat16),
    }
    nc = bacc.Bacc("TRN2", target_bir_lowering=False, num_devices=1)
    args = [nc.dram_tensor(f"{n}_dram", a.shape, mb.dt.from_np(a.dtype), kind="ExternalInput").ap() for n, a in arrays.items()]
    out = nc.dram_tensor("out_dram", (N, C), mb.dt.float32, kind="ExternalOutput").ap()
    build_mingru_top1_moe(nc, *args, out)
    r = run_bass_kernel_spmd(nc, [{f"{n}_dram": a for n, a in arrays.items()}], core_ids=[0])
    return r.results[0]["out_dram"].reshape(B, S, C)
```

```python
import concourse.bass as bass
from concourse import mybir
from contextlib import ExitStack

B, S, C = 8, 512, 128
E, H, R = 8, 256, 16
P = 128
LOG_P = P.bit_length() - 1
N = B * S
TB = S // P
G = 2
BG = B // G
TG = BG * TB
NG = TG * P
SG = (NG + E * (P - 1)) // P
MAIN = TG + E // 2
REST = SG - MAIN
QG = MAIN // 2
Q = G * QG
assert MAIN % 4 == 0
LN_EPS = 1e-5
NORM_MIN = 1e-4

CF_IDENT = 0
CF_DESC = CF_IDENT + P
CF_RESET = CF_DESC + TG * E
CF_TILE_E = CF_RESET + TG * E
CF_END = CF_TILE_E + SG * E
GW_WZ, GW_WH, GW_BZ, GW_BH, GW_END = 0, C, 2 * C, 2 * C + 1, 2 * C + 2
RW_RED, RW_WG, RW_END = 0, C, C + E
CB_BEFORE = 0
CB_ONES = CB_BEFORE + P
CB_END = CB_ONES + P
assert NG <= 2048
CH_COUNT = 0
CH_TOKEN = CH_COUNT + P * TG
CH_END = CH_TOKEN + SG * TG


def build_mingru_top1_moe(nc, xT_d, gate_w_d, router_w_d, w1_d, b1_d, w2_d, b2_d, cf_d, cb_d, ch_d, out_d):
    f32, f16, bf16, i32, u32 = mybir.dt.float32, mybir.dt.float16, mybir.dt.bfloat16, mybir.dt.int32, mybir.dt.uint32
    ALU = mybir.AluOpType
    ACT = mybir.ActivationFunctionType
    AX = mybir.AxisListType

    x1_dram = [nc.dram_tensor(f"x1_rows_{g}", (NG, C), f32).ap() for g in range(G)]
    o_dram = [nc.dram_tensor(f"expert_out_rows_{g}", (SG * P, C), f32).ap() for g in range(G)]

    ctx = ExitStack()
    with ctx:
        def sb(name, shape, dt=f32):
            return ctx.enter_context(nc.sbuf_tensor(name, shape, dt))

        def sem(name):
            return ctx.enter_context(nc.semaphore(name))

        RING, RING4 = 2, 4
        xT = sb("xT", [P, N])
        gate_w = sb("gate_w", [P, GW_END])
        wz, wh = gate_w[:, GW_WZ:GW_WZ + C], gate_w[:, GW_WH:GW_WH + C]
        bz, bh = gate_w[:, GW_BZ:GW_BZ + 1], gate_w[:, GW_BH:GW_BH + 1]
        gate_bias = sb("gate_bias", [P, 2])
        cf = sb("cf", [P, CF_END])
        cb = sb("cb", [P, CB_END], bf16)
        ch = sb("ch", [P, CH_END], f16)
        warm_act = sb("warm_act", [P, 1])
        w1 = sb("w1", [P, E * H])
        w2 = sb("w2", [P, E, H // P, C])
        keep = sb("keep", [P, RING, S])
        z = sb("z", [P, RING, S])
        sg = sb("sg", [P, RING, S])
        cand = sb("cand", [P, RING, S])
        zcand = sb("zcand", [P, RING, S])
        h = sb("h", [P, RING4, S])
        sT = sb("sT", [P, RING4, S])
        st1 = sb("st1", [P, RING, TB, 6])
        mv = sb("mv", [P, B * TB, 2])
        var1 = sb("var1", [P, B * TB])
        rstd = sb("rstd", [P, B * TB])
        nmean = sb("nmean", [P, B * TB])
        nmr = sb("nmr", [P, B * TB])
        x1 = sb("x1", [P, B * TB, C])
        router_w = sb("router_w", [R, RW_END])
        wredT, wgT = router_w[:, RW_RED:RW_RED + C], router_w[:, RW_WG:RW_WG + E]
        wredc = sb("wredc", [R, C])
        wg_sq = sb("wg_sq", [R, E])
        red_mean = sb("red_mean", [R, 2])
        norm_sq = sb("norm_sq", [P, E])
        inv_norm = sb("inv_norm", [P, E])
        ones16 = sb("ones16", [R, P])
        half = sb("half", [P, TG])
        router = sb("router", [P, E])
        b1 = sb("b1", [P, E * H // P])
        b2 = sb("b2", [P, E * C])
        mx = sb("mx", [P, TG])
        gap = sb("gap", [P, G, TG, E])
        key = sb("key", [P, TG, E])
        kmx = sb("kmx", [P, TG])
        oh = sb("oh", [P, E, TG], bf16)
        incl = sb("incl", [P, E, TG], bf16)
        cnt = sb("cnt", [P, 2, E], i32)
        ends = sb("ends", [P, E])
        base = sb("base", [P, E])
        rsel = sb("rsel", [P, E, TG])
        bsel = sb("bsel", [P, E, TG])
        tok_rank = sb("tok_rank", [P, TG], u32)
        tok_base = sb("tok_base", [P, TG])
        slot = sb("slot", [P, G, TG], u32)
        lane = sb("lane", [P, TG], u32)
        lane16 = sb("lane16", [P, TG], f16)
        rtile = sb("rtile", [P, TG], u32)
        tile_of = sb("tile_of", [P, TG], f16)
        ohB = sb("ohB", [P, P, TG], f16)
        ohA = sb("ohA", [P, SG, TG], f16)
        rhsA = sb("rhsA", [P, SG, TG], f16)
        gidx = sb("gidx", [P, G, SG], u32)
        tcmp = sb("tcmp", [P, SG, E])
        tsum = sb("tsum", [P, SG])
        texp = sb("texp", [P, G, SG + 1], i32)
        sgap = sb("sgap", [P, TG, E])
        sp_ = sb("sp_", [P, TG, E])
        sn_ = sb("sn_", [P, TG, E])
        rn_ = sb("rn_", [P, TG, E])
        den = sb("den", [P, TG])
        score = sb("score", [P, G, TG])
        xg = sb("xg", [P, G * SG, C])
        xgT = sb("xgT", [P, RING, 2 * P])
        w1x = sb("w1x", [P, RING4, 2, H])
        hgT = sb("hgT", [P, RING, 2, H // P, P])
        osb = sb("osb", [P, G * SG, C])
        og = sb("og", [P, B * TB, C])
        st2 = sb("st2", [P, B * TB, 6])
        mv2 = sb("mv2", [P, B * TB, 2])
        eps = sb("eps", [P, 1])
        dev2 = sb("dev2", [P, B * TB])
        rstd2 = sb("rstd2", [P, B * TB])
        nmr2 = sb("nmr2", [P, B * TB])
        y = og

        bank = [ctx.enter_context(nc.psum_tensor(f"bank{i}", [P, 512], f32)) for i in range(8)]
        k_ps, pre_ps, s_ps = bank[0:2], bank[2:4], bank[4:6]
        logit_ps, route_ps = bank[6], bank[7]
        xT_ps, hT_ps, o_ps = bank[0:2], bank[2:4], bank[4:6]
        RANK, COUNT, TABLE = 0, 128, 160

        ld_gate, ld_rt, ld_cf, ld_cb, ld_ch, ld_w1, ld_w2, ld_b1, ld_b2 = (sem(n) for n in (
            "gate_weights_loaded", "router_weights_loaded", "constants_loaded", "bf16_constants_loaded",
            "f16_constants_loaded", "w1_loaded", "w2_loaded", "b1_loaded", "b2_loaded"))
        ld_x = [sem(f"x_loaded_{s}") for s in range(B)]
        gbias_ready = sem("gate_bias_ready")
        half_ready = sem("half_ready")
        rt_dve, rt_pe = sem("router_dve"), sem("router_pe")
        norm_ready, inv_norm_ready = sem("router_norms_ready"), sem("router_inverse_norms_ready")
        router_ready = sem("router_ready")
        k_done, pre_done = sem("k_done"), sem("pre_done")
        z_done, sg_done = sem("z_keep_done"), sem("sg_done")
        cand_done, zcand_done, h_done = sem("cand_done"), sem("zcand_done"), sem("h_done")
        s_done, stok_done, logit_done = sem("s_done"), sem("s_tokens_done"), sem("logits_done")
        st_done, mv_done = sem("stats_done"), sem("mean_var_done")
        pool_ln, rstd_done, x1_done = sem("pool_ln_chain"), sem("rstd_done"), sem("x1_done")
        s_late, s_kept = sem("s_late_done"), sem("s_tokens_kept")
        var_late, rstd_late, nmr_late = sem("late_variances_done"), sem("late_rstd_done"), sem("late_mean_rstd_done")
        x1_dve = sem("x1_of_vector_done")
        x1_stored = [sem(f"x1_stored_{g}") for g in range(G)]
        gap_done = sem("gap_done")
        rc, te = sem("route_chain"), sem("tile_expert_chain")
        rk, bs, rhs_ready, lane_ready = (sem(n) for n in (
            "rank_chain", "base_chain", "table_rhs_ready", "lane_ready"))
        incl_done, rank_done, lanes_done, table_done = sem("incl_done"), sem("rank_done"), sem("lanes_done"), sem("table_done")
        gidx_done, texp_done = sem("gather_index_done"), sem("tile_expert_done")
        slot_done = sem("slot_done")
        sgap_done, sig_done, score_done = sem("score_gap_done"), sem("score_sigmoids_done"), sem("score_done")
        sc = sem("score_chain")
        xg_done = [sem(f"x_gathered_{i}") for i in range(4)]
        xT_done, xgT_done, up_done, gelu_done = sem("x_transposed"), sem("xgT_copied"), sem("up_done"), sem("gelu_done")
        w1x_first, w1x_done, down_done, o_done = sem("w1_of_first_tiles_copied"), sem("w1_of_tiles_copied"), sem("down_done"), sem("o_copied")
        o_stored = [sem(f"o_stored_{g}") for g in range(G)]
        rest_zero, o_zeroed = sem("rest_zero"), [sem(f"o_rest_zeroed_{g}") for g in range(G)]
        r_x, r_xT, r_xgT, r_w1, r_up, r_gelu, r_down, r_o, r_stored = ([sem(f"rest_{n}_{g}") for g in range(G)] for n in (
            "x_gathered", "x_transposed", "xgT_copied", "w1_copied", "up_done", "gelu_done", "down_done", "o_copied", "o_stored"))
        og_done = [sem(f"o_gathered_{i}") for i in range(4)]
        res_done, st2_done, mv2_done, rstd2_done = sem("residual_done"), sem("stats2_done"), sem("mean_var2_done"), sem("rstd2_done")
        eps_ready, dev2_done = sem("eps_ready"), sem("deviations2_done")
        nmr2_done = sem("mean_rstd2_done")
        y_done, y_last, out_stored = sem("y_done"), sem("last_y_done"), sem("out_stored")

        LAG = 2
        VECTOR_ADDS = range(BG - 1, B)
        POOL_ADDS = range(BG - 1)
        added = lambda s: (s_late, VECTOR_ADDS.index(s) + 1) if s in VECTOR_ADDS else (s_done, POOL_ADDS.index(s) + 1)
        first_tile = lambda q: (q // QG) * SG + 2 * (q % QG)
        tok = lambda s: slice(s * S, (s + 1) * S)
        tiles = lambda s: slice(s * TB, (s + 1) * TB)

        landed = lambda q: 32 * (q // 4 + 1)
        NORM_TILES = [(t, t + TB) for t in range(0, B * TB, TB)]

        def used_tiles(engine, eng, g):
            eng.wait_ge(texp_done, g + 1)
            _, used = nc.values_load_multi_w_load_instructions(
                texp[0:1, g, SG:SG + 1], engines=[engine], min_val=0, max_val=SG,
                skip_runtime_bounds_check_because="VectorE's count is between TG and SG")
            return used[0]

        def rest_experts(engine, g):
            _, e = nc.values_load_multi_w_load_instructions(
                texp[0:1, g, MAIN:SG], engines=[engine], min_val=0, max_val=E - 1,
                skip_runtime_bounds_check_because="VectorE takes the minimum with E - 1 of a count that is never negative")
            return e

        block = ctx.enter_context(nc.Block())

        @block.sync
        def _(sp):
            sp.dma_start(gate_w[:, :], gate_w_d).then_inc(ld_gate, 16)
            sp.dma_start(xT[:, tok(0)], xT_d[:, tok(0)]).then_inc(ld_x[0], 16)
            sp.dma_start(router_w[:, :], router_w_d).then_inc(ld_rt, 16)
            for s in range(1, B):
                sp.dma_start(xT[:, tok(s)], xT_d[:, tok(s)]).then_inc(ld_x[s], 16)
                if s == 1:
                    sp.dma_start(cf[:, :], cf_d).then_inc(ld_cf, 16)
                if s == 3:
                    sp.dma_start(cb[:, :], cb_d).then_inc(ld_cb, 16)
                    sp.dma_start(ch[:, :], ch_d).then_inc(ld_ch, 16)
            sp.dma_start(w1[:, :].rearrange("c (e h) -> c e h", e=E), w1_d.rearrange("e c h -> c e h")).then_inc(ld_w1, 16)
            sp.dma_start(w2[:, :, :, :], w2_d.rearrange("e (k p) c -> p e k c", p=P)).then_inc(ld_w2, 16)
            sp.dma_start(b1[:, :], b1_d).then_inc(ld_b1, 16)
            sp.dma_start(b2[:, :], b2_d.rearrange("e c -> (e c)").partition_broadcast(P)).then_inc(ld_b2, 16)
            sp.wait_ge(rest_zero, G)
            for g in range(G):
                sp.dma_start(o_dram[g][MAIN * P:, :].rearrange("(t p) c -> p t c", p=P),
                             osb[:, g * SG + MAIN:(g + 1) * SG, :]).then_inc(o_zeroed[g], 16)
            for s in range(B):
                g, t0 = s // BG, (s % BG) * TB
                if s < B - 1:
                    sp.wait_ge(x1_done, s + 1)
                if s == 0:
                    sp.wait_ge(x1_dve, 1)
                if s == B - 1:
                    sp.wait_ge(x1_dve, 2)
                sp.dma_start(x1_dram[g][t0 * P:(t0 + TB) * P, :].rearrange("(t p) c -> p t c", p=P),
                             x1[:, tiles(s), :]).then_inc(x1_stored[g], 16)

            def store_pair(q):
                g, a = q // QG, 2 * (q % QG)
                sp.wait_ge(o_done, q + 1)
                sp.dma_start(o_dram[g][a * P:(a + 2) * P, :].rearrange("(t p) c -> p t c", p=P),
                             osb[:, first_tile(q):first_tile(q) + 2, :]).then_inc(o_stored[g], 16)

            def store_rest(g):
                with sp.If(used_tiles(mybir.EngineType.SP, sp, g) > MAIN):
                    sp.wait_ge(o_zeroed[g], 16)
                    for i in range(REST):
                        sp.wait_ge(r_o[g], i + 1)
                        sp.dma_start(o_dram[g][(MAIN + i) * P:(MAIN + i + 1) * P, :], osb[:, g * SG + MAIN + i, :]).then_inc(r_stored[g], 16)

            def store_out(t, n):
                if t < NORM_TILES[-1][0]:
                    sp.wait_ge(y_done, t + n)
                else:
                    sp.wait_ge(y_last, t + n - NORM_TILES[-1][0])
                sp.dma_start(out_d[t * P:(t + n) * P, :].rearrange("(t p) c -> p t c", p=P), y[:, t:t + n, :]).then_inc(out_stored, 16)

            for q in range(Q):
                store_pair(q)
            for g in range(G):
                store_rest(g)
            parts = [TB] * (B - 2) + [TB // 2, TB // 2, TB - 1, 1]
            for i, n in enumerate(parts):
                store_out(sum(parts[:i]), n)
            sp.wait_ge(out_stored, 16 * len(parts))

        @block.tensor
        def _(pe):
            ident = cf[:, CF_IDENT:CF_IDENT + P]

            def gates(s):
                if s == 0:
                    pe.wait_ge(ld_gate, 16)
                pe.wait_ge(ld_x[s], 16)
                if s >= 2:
                    pe.wait_ge(z_done, s - 1)
                    pe.wait_ge(cand_done, s - 1)
                nc.tensor.matmul(pre_ps[s % 2][:, :], wh, xT[:, tok(s)], start=True, stop=True).then_inc(pre_done, 1)
                nc.tensor.matmul(k_ps[s % 2][:, :], wz, xT[:, tok(s)], start=True, stop=True).then_inc(k_done, 1)

            def router_weights():
                pe.wait_ge(rt_dve, 4)
                nc.tensor.matmul(route_ps[:, 0:E], ones16[:, :], wg_sq[:, :], start=True, stop=True)
                nc.tensor.matmul(route_ps[:, E:2 * E], wredc[:, :], wgT, start=True, stop=True).then_inc(rt_pe, 1)

            def to_tokens(s):
                if s >= 2:
                    pe.wait_ge(s_kept, s - 1)
                for j in range(TB):
                    last = nc.tensor.transpose(s_ps[s % 2][:, j * P:(j + 1) * P], sT[:, s % RING4, j * P:(j + 1) * P], ident)
                last.then_inc(stok_done, 1)

            def logits(s):
                if s == 0:
                    pe.wait_ge(router_ready, 1)
                if s % BG == 0 and s:
                    pe.wait_ge(gap_done, s // BG)
                for j in range(TB):
                    t = (s % BG) * TB + j
                    last = nc.tensor.matmul(logit_ps[:, t * E:(t + 1) * E], sT[:, s % RING4, j * P:(j + 1) * P],
                                            router[:, :], start=True, stop=True)
                last.then_inc(logit_done, 1)

            def tokens(s):
                pe.wait_ge(*added(s))
                if s == 0:
                    pe.wait_ge(ld_cf, 16)
                to_tokens(s)
                logits(s)

            def rank(g):
                pe.wait_ge(incl_done, g + 1)
                if g == 0:
                    pe.wait_ge(ld_cb, 16)
                if g:
                    pe.wait_ge(gidx_done, g)
                flat_oh = oh[:, :, :].rearrange("p e t -> p (e t)")
                flat_incl = incl[:, :, :].rearrange("p e t -> p (e t)")
                nc.tensor.matmul(route_ps[:, RANK:RANK + E * TG], cb[:, CB_BEFORE:CB_BEFORE + P], flat_oh, start=True, stop=False)
                nc.tensor.matmul(route_ps[:, RANK:RANK + E * TG], cb[:, CB_ONES:CB_ONES + P], flat_incl, start=False, stop=True)
                nc.tensor.matmul(route_ps[:, COUNT:COUNT + E], cb[:, CB_ONES:CB_ONES + P], incl[:, :, TG - 1],
                                 start=True, stop=True).then_inc(rank_done, 1)

            def table(g):
                pe.wait_ge(rhs_ready, g + 1)
                pe.wait_ge(lanes_done, g + 1)
                for t in range(TG):
                    last = nc.tensor.matmul(route_ps[:, TABLE:TABLE + SG], ohB[:, :, t], rhsA[:, :, t],
                                            start=(t == 0), stop=(t == TG - 1))
                last.then_inc(table_done, 1)

            def x_transpose(q):
                if q < 2:
                    pe.wait_ge(z_done, B - 1 + q)
                pe.wait_ge(xg_done[q % 4], landed(q))
                if q >= 2:
                    pe.wait_ge(xgT_done, q - 1)
                for j in range(2):
                    last = nc.tensor.transpose(xT_ps[q % 2][:, j * P:(j + 1) * P], xg[:, first_tile(q) + j, :], ident)
                last.then_inc(xT_done, 1)

            def experts(q):
                g, a = q // QG, 2 * (q % QG)
                if q % QG == 0:
                    pe.wait_ge(texp_done, g + 1)
                _, e = nc.values_load_multi_w_load_instructions(
                    texp[0:1, g, a:a + 4], engines=[mybir.EngineType.PE], min_val=0, max_val=E - 1,
                    skip_runtime_bounds_check_because="VectorE takes the minimum with E - 1 of a count that is never negative")
                return {q: e[0:2], q + 1: e[2:4]}

            def up(q):
                pe.wait_ge(xgT_done, q + 1)
                if q < 2:
                    pe.wait_ge(w1x_first, q + 1)
                    pe.wait_ge(cand_done, B - 1 + q)
                else:
                    pe.wait_ge(w1x_done, q - 1)
                if q >= 2:
                    pe.wait_ge(gelu_done, q - 1)
                for j in range(2):
                    for k in range(H // P):
                        o = hT_ps[q % 2][:, (j * (H // P) + k) * P:(j * (H // P) + k + 1) * P]
                        last = nc.tensor.matmul(o, w1x[:, q % RING4, j, k * P:(k + 1) * P], xgT[:, q % 2, j * P:(j + 1) * P],
                                                start=True, stop=True)
                last.then_inc(up_done, 1)

            w2f = w2[:, :, :, :].rearrange("p e k c -> p (e k c)")

            def down(q, e):
                pe.wait_ge(gelu_done, q + 1)
                if q == 0:
                    pe.wait_ge(ld_w2, 16)
                if q < 2:
                    pe.wait_ge(s_kept, B - 1 + q)
                if q >= 2:
                    pe.wait_ge(o_done, q - 1)
                for j in range(2):
                    o = o_ps[q % 2][:, j * C:(j + 1) * C]
                    for k in range(H // P):
                        last = nc.tensor.matmul(o, hgT[:, q % 2, j, k, :], w2f[:, bass.ds(e[j] * H + k * C, C)],
                                                start=(k == 0), stop=(k == H // P - 1))
                last.then_inc(down_done, 1)

            def rest(g):
                with pe.If(used_tiles(mybir.EngineType.PE, pe, g) > MAIN):
                    e = rest_experts(mybir.EngineType.PE, g)
                    pe.wait_ge(o_done, Q)
                    pe.wait_ge(r_x[g], 16 * REST)
                    for i in range(REST):
                        nc.tensor.transpose(xT_ps[0][:, 0:P], xg[:, g * SG + MAIN + i, :], ident).then_inc(r_xT[g], 1)
                        pe.wait_ge(r_xgT[g], i + 1)
                        pe.wait_ge(r_w1[g], i + 1)
                        for k in range(H // P):
                            last = nc.tensor.matmul(hT_ps[0][:, k * P:(k + 1) * P], w1x[:, 0, 0, k * P:(k + 1) * P], xgT[:, 0, 0:P],
                                                    start=True, stop=True)
                        last.then_inc(r_up[g], 1)
                        pe.wait_ge(r_gelu[g], i + 1)
                        for k in range(H // P):
                            last = nc.tensor.matmul(o_ps[0][:, 0:C], hgT[:, 0, 0, k, :], w2f[:, bass.ds(e[i] * H + k * C, C)],
                                                    start=(k == 0), stop=(k == H // P - 1))
                        last.then_inc(r_down[g], 1)
                        pe.wait_ge(r_o[g], i + 1)

            gates(0)
            router_weights()
            for s in range(1, B):
                if s == BG + 1:
                    tokens(BG - 1)
                    rank(0)
                gates(s)
                if s == BG + 1:
                    table(0)
                elif s >= LAG:
                    tokens(s - LAG)
            tokens(B - 2)
            x_transpose(0)
            x_transpose(1)
            up(0)
            tokens(B - 1)
            rank(1)
            up(1)
            x_transpose(2)
            e_of = experts(0)
            down(0, e_of[0])
            x_transpose(3)
            up(2)
            down(1, e_of[1])
            x_transpose(4)
            table(1)
            up(3)
            e_of = experts(2)
            down(2, e_of[2])
            for q in range(3, Q):
                if q + 2 < Q:
                    x_transpose(q + 2)
                if q + 1 < Q:
                    up(q + 1)
                if q % 2 == 0:
                    e_of = experts(q)
                down(q, e_of[q])
            for g in range(G):
                rest(g)

        @block.scalar
        def _(act):
            def sigmoids(s):
                if s == 0:
                    act.wait_ge(gbias_ready, 2)
                if s >= 2:
                    act.wait_ge(h_done, s - 1)
                act.wait_ge(pre_done, s + 1)
                nc.scalar.activation(sg[:, s % 2, :], pre_ps[s % 2][:, :], ACT.Sigmoid, bias=bh).then_inc(sg_done, 1)
                act.wait_ge(k_done, s + 1)
                nc.scalar.activation(z[:, s % 2, :], k_ps[s % 2][:, :], ACT.Sigmoid, bias=bz)
                nc.scalar.activation(keep[:, s % 2, :], k_ps[s % 2][:, :], ACT.Sigmoid, bias=gate_bias[:, 0:1], scale=-1.0).then_inc(z_done, 1)

            def keep_tokens(s):
                act.wait_ge(stok_done, s + 1)
                nc.scalar.copy(x1[:, tiles(s), :].rearrange("p t c -> p (t c)"), s_ps[s % 2][:, :]).then_inc(s_kept, 1)

            def normalize(s):
                if s < BG:
                    act.wait_ge(rstd_done, s + 1)
                else:
                    act.wait_ge(nmr_late, (s - BG) // 2 + 1)
                for t in range(s * TB, TB // 2 if s == 0 else (s + 1) * TB):
                    last = nc.scalar.activation(x1[:, t, :], x1[:, t, :], ACT.Identity, bias=nmr[:, t:t + 1], scale=rstd[:, t:t + 1])
                last.then_inc(x1_done, 1)

            def score_sigmoids(g):
                act.wait_ge(sgap_done, g + 1)
                nc.scalar.activation(sp_[:, :, :], sgap[:, :, :], ACT.Sigmoid)
                nc.scalar.activation(sn_[:, :, :], sgap[:, :, :], ACT.Sigmoid, scale=-1.0).then_inc(sig_done, 1)

            def deviations(n):
                a, b = NORM_TILES[n]
                act.wait_ge(mv2_done, b)
                nc.scalar.activation(dev2[:, a:b], mv2[:, a:b, 1], ACT.Sqrt, bias=eps[:, 0:1]).then_inc(dev2_done, 1)

            def normalize2(n, part=slice(0, TB)):
                act.wait_ge(nmr2_done, n + 1)
                for t in range(*NORM_TILES[n])[part]:
                    nc.scalar.activation(y[:, t, :], og[:, t, :], ACT.Identity, bias=nmr2[:, t:t + 1],
                                         scale=rstd2[:, t:t + 1]).then_inc(y_done, 1)

            def copy_xT(q):
                act.wait_ge(xT_done, q + 1)
                if q >= 2:
                    act.wait_ge(up_done, q - 1)
                nc.scalar.copy(xgT[:, q % 2, 0:2 * P], xT_ps[q % 2][:, 0:2 * P]).then_inc(xgT_done, 1)

            def experts(q):
                g, a = q // QG, 2 * (q % QG)
                if q % QG == 0:
                    act.wait_ge(texp_done, g + 1)
                _, e = nc.values_load_multi_w_load_instructions(
                    texp[0:1, g, a:a + 4], engines=[mybir.EngineType.Activation], min_val=0, max_val=E - 1,
                    skip_runtime_bounds_check_because="VectorE takes the minimum with E - 1 of a count that is never negative")
                return {q: e[0:2], q + 1: e[2:4]}

            def copy_w1(q, e):
                act.wait_ge(ld_w1, 16)
                for j in range(2):
                    last = nc.scalar.copy(w1x[:, q % RING4, j, :], w1[:, bass.ds(e[j] * H, H)])
                last.then_inc(w1x_first, 1)

            def gelu(q, e):
                act.wait_ge(up_done, q + 1)
                if q == 0:
                    act.wait_ge(ld_b1, 16)
                if q >= 2:
                    act.wait_ge(down_done, q - 1)
                for j in range(2):
                    for k in range(H // P):
                        last = nc.scalar.activation(hgT[:, q % 2, j, k, :], hT_ps[q % 2][:, (j * (H // P) + k) * P:(j * (H // P) + k + 1) * P],
                                                    ACT.Gelu, bias=b1[:, bass.ds(e[j] * (H // P) + k, 1)])
                last.then_inc(gelu_done, 1)

            def rest(g):
                with act.If(used_tiles(mybir.EngineType.Activation, act, g) > MAIN):
                    e = rest_experts(mybir.EngineType.Activation, g)
                    for i in range(REST):
                        act.wait_ge(r_xT[g], i + 1)
                        nc.scalar.copy(xgT[:, 0, 0:P], xT_ps[0][:, 0:P]).then_inc(r_xgT[g], 1)
                        act.wait_ge(r_up[g], i + 1)
                        for k in range(H // P):
                            last = nc.scalar.activation(hgT[:, 0, 0, k, :], hT_ps[0][:, k * P:(k + 1) * P], ACT.Gelu,
                                                        bias=b1[:, bass.ds(e[i] * (H // P) + k, 1)])
                        last.then_inc(r_gelu[g], 1)

            act.wait_ge(eps_ready, 1)
            nc.scalar.activation(warm_act[:, :], eps[:, :], ACT.Sigmoid)
            for s in range(B):
                if s == BG + 1:
                    keep_tokens(BG - 1)
                    for n in range(BG):
                        normalize(n)
                sigmoids(s)
                if s == BG + 1:
                    score_sigmoids(0)
                elif s >= LAG:
                    keep_tokens(s - LAG)
            nc.scalar.activation(warm_act[:, :], eps[:, :], ACT.Gelu)
            e_of = experts(0)
            copy_w1(0, e_of[0])
            copy_xT(0)
            copy_w1(1, e_of[1])
            copy_xT(1)
            keep_tokens(B - 2)
            keep_tokens(B - 1)
            normalize(BG)
            gelu(0, e_of[0])
            normalize(BG + 1)
            copy_xT(2)
            normalize(BG + 2)
            gelu(1, e_of[1])
            copy_xT(3)
            e_of = experts(2)
            gelu(2, e_of[2])
            copy_xT(4)
            for q in range(3, Q):
                if q % 2 == 0:
                    e_of = experts(q)
                gelu(q, e_of[q])
                if q + 2 < Q:
                    copy_xT(q + 2)
            for g in range(G):
                rest(g)
            score_sigmoids(1)
            nc.scalar.activation(warm_act[:, :], eps[:, :], ACT.Sqrt)
            for n in range(len(NORM_TILES)):
                deviations(n)
                if n < len(NORM_TILES) - 2:
                    normalize2(n)
                elif n == len(NORM_TILES) - 2:
                    normalize2(n, slice(0, TB // 2))
            normalize2(len(NORM_TILES) - 2, slice(TB // 2, TB))

        @block.gpsimd
        def _(pool):
            nc.gpsimd.memset(half[:, :], -0.5).then_inc(half_ready, 1)
            nc.gpsimd.memset(eps[:, :], LN_EPS).then_inc(eps_ready, 1)
            for g in range(G):
                nc.gpsimd.memset(osb[:, g * SG + MAIN:(g + 1) * SG, :], 0.0).then_inc(rest_zero, 1)
            pool.wait_ge(half_ready, 1)
            pool.wait_ge(norm_ready, 1)
            nc.gpsimd.tensor_tensor(inv_norm[:, :], norm_sq[:, :], half[:, 0:E], ALU.pow).then_inc(inv_norm_ready, 1)

            def add_input(s):
                pool.wait_ge(h_done, s + 1)
                nc.gpsimd.tensor_tensor(sT[:, s % RING4, :], h[:, s % RING4, :], xT[:, tok(s)], ALU.add).then_inc(s_done, 1)

            def inverse_deviations(n, s, end):
                ts = slice(s * TB, end * TB)
                pool.wait_ge(mv_done, end)
                nc.gpsimd.tensor_scalar(var1[:, ts], mv[:, ts, 1], LN_EPS, None, ALU.add).then_inc(pool_ln, 1)
                nc.gpsimd.tensor_scalar(nmean[:, ts], mv[:, ts, 0], -1.0, None, ALU.mult)
                pool.wait_ge(pool_ln, 2 * n + 1)
                nc.gpsimd.tensor_tensor(rstd[:, ts], var1[:, ts], half[:, 0:(end - s) * TB], ALU.pow).then_inc(pool_ln, 1)
                pool.wait_ge(pool_ln, 2 * n + 2)
                nc.gpsimd.tensor_tensor(nmr[:, ts], nmean[:, ts], rstd[:, ts], ALU.mult).then_inc(rstd_done, end - s)

            def gather_tokens(q):
                g = q // QG
                if q % QG == 0:
                    pool.wait_ge(gidx_done, g + 1)
                    pool.wait_ge(x1_stored[g], 16 * BG)
                if q >= 4:
                    pool.wait_ge(xg_done[q % 4], landed(q - 4))
                for j in range(2):
                    a = 2 * (q % QG) + j
                    nc.gpsimd.indirect_dma_start(out=xg[:, first_tile(q) + j, :], out_offset=None, in_=x1_dram[g],
                                                 in_offset=bass.IndirectOffsetOnAxis(ap=gidx[:, g, a:a + 1], axis=0)
                                                 ).then_inc(xg_done[q % 4], 16)

            def gather_outputs(i):
                g, t = i // TG, i % TG
                if t == 0:
                    pool.wait_ge(slot_done, g + 1)
                    pool.wait_ge(o_zeroed[g], 16)
                    pool.wait_ge(o_stored[g], 16 * QG)
                    with pool.If(used[g] > MAIN):
                        pool.wait_ge(r_stored[g], 16 * REST)
                if i >= 4:
                    pool.wait_ge(og_done[i % 4], 16 * (i // 4))
                nc.gpsimd.indirect_dma_start(out=og[:, i, :], out_offset=None, in_=o_dram[g],
                                             in_offset=bass.IndirectOffsetOnAxis(ap=slot[:, g, t:t + 1], axis=0)).then_inc(og_done[i % 4], 16)

            def late_inverse(s):
                ts = slice(s * TB, (s + 2) * TB)
                pool.wait_ge(var_late, (s - BG) // 2 + 1)
                nc.gpsimd.tensor_tensor(rstd[:, ts], var1[:, ts], half[:, 0:2 * TB], ALU.pow).then_inc(rstd_late, 1)
                pool.wait_ge(rstd_late, (s - BG) // 2 + 1)
                nc.gpsimd.tensor_tensor(nmr[:, ts], nmean[:, ts], rstd[:, ts], ALU.mult).then_inc(nmr_late, 1)

            for s in range(BG - 1):
                add_input(s)
            inverse_deviations(0, 0, 2)
            inverse_deviations(1, 2, 3)
            inverse_deviations(2, 3, 4)
            for q in range(Q):
                gather_tokens(q)
                if q == 5:
                    late_inverse(BG)
                if q == 7:
                    late_inverse(BG + 2)
            used = [used_tiles(mybir.EngineType.Pool, pool, g) for g in range(G)]
            for g in range(G):
                with pool.If(used[g] > MAIN):
                    for a in range(MAIN, SG):
                        nc.gpsimd.indirect_dma_start(out=xg[:, g * SG + a, :], out_offset=None, in_=x1_dram[g],
                                                     in_offset=bass.IndirectOffsetOnAxis(ap=gidx[:, g, a:a + 1], axis=0)
                                                     ).then_inc(r_x[g], 16)
            for i in range(B * TB):
                gather_outputs(i)

        @block.vector
        def _(dve):
            dve.wait_ge(ld_gate, 16)
            nc.vector.tensor_scalar(gate_bias[:, 0:1], bz, -1.0, None, ALU.mult).then_inc(gbias_ready, 1)
            nc.vector.tensor_scalar(gate_bias[:, 1:2], bh, 0.5, None, ALU.add).then_inc(gbias_ready, 1)
            dve.wait_ge(gbias_ready, 2)

            def router_weights():
                nc.vector.memset(ones16[:, :], 1.0).then_inc(rt_dve, 1)
                dve.wait_ge(ld_rt, 16)
                nc.vector.reduce_sum(red_mean[:, 0:1], wredT, AX.X).then_inc(rt_dve, 1)
                dve.wait_ge(rt_dve, 2)
                nc.vector.tensor_scalar(red_mean[:, 1:2], red_mean[:, 0:1], 1.0 / C, None, ALU.mult).then_inc(rt_dve, 1)
                nc.vector.tensor_tensor(wg_sq[:, :], wgT, wgT, ALU.mult)
                dve.wait_ge(rt_dve, 3)
                nc.vector.tensor_scalar(wredc[:, :], wredT, red_mean[:, 1:2], None, ALU.subtract).then_inc(rt_dve, 1)

            def router_norms():
                dve.wait_ge(rt_pe, 1)
                nc.vector.tensor_scalar(norm_sq[:, :], route_ps[:, 0:E], NORM_MIN * NORM_MIN, None, ALU.max).then_inc(norm_ready, 1)

            def scale_router():
                dve.wait_ge(inv_norm_ready, 1)
                nc.vector.tensor_tensor(router[:, :], route_ps[:, E:2 * E], inv_norm[:, :], ALU.mult).then_inc(router_ready, 1)

            ROUTE, TILE_E, RK, BS = 4, 3, 3, 9

            def candidate(s):
                dve.wait_ge(sg_done, s + 1)
                nc.vector.scalar_tensor_tensor(out=cand[:, s % 2, :], in0=pre_ps[s % 2][:, :], scalar=gate_bias[:, 1:2],
                                               in1=sg[:, s % 2, :], op0=ALU.add, op1=ALU.max).then_inc(cand_done, 1)

            def gated(s):
                dve.wait_ge(z_done, s + 1)
                dve.wait_ge(cand_done, s + 1)
                nc.vector.tensor_tensor(zcand[:, s % 2, :], z[:, s % 2, :], cand[:, s % 2, :], ALU.mult).then_inc(zcand_done, 1)

            def scan(s):
                dve.wait_ge(zcand_done, s + 1)
                if s >= RING4:
                    dve.wait_ge(*added(s - RING4))
                nc.vector.tensor_tensor_scan(h[:, s % RING4, :], keep[:, s % 2, :], zcand[:, s % 2, :], 0.5,
                                             ALU.mult, ALU.add).then_inc(h_done, 1)

            def add_input(s):
                dve.wait_ge(h_done, s + 1)
                if s >= RING4:
                    dve.wait_ge(logit_done, s - RING4 + 1)
                nc.vector.tensor_tensor(sT[:, s % RING4, :], h[:, s % RING4, :], xT[:, tok(s)], ALU.add).then_inc(s_late, 1)

            def stat_tile(s, j):
                ins = nc.vector.bn_stats(st1[:, s % 2, j, :], x1[:, s * TB + j, :])
                if j == TB - 1:
                    ins.then_inc(st_done, 1)

            def stats(s):
                dve.wait_ge(s_kept, s + 1)
                for j in range(TB):
                    stat_tile(s, j)

            def mean_var(s):
                dve.wait_ge(st_done, s + 1)
                for j in range(TB):
                    last = nc.vector.bn_aggr(mv[:, s * TB + j, :], st1[:, s % 2, j, :])
                last.then_inc(mv_done, 1)

            def tile_cols(c, n, w):
                return cf[:, c:c + n * w].rearrange("p (t a) -> p t a", a=w)

            def over(ap, n):
                return ap.unsqueeze(2).to_broadcast([P, ap.shape[1], n])

            def route_experts(g):
                s = BG * (g + 1) - 1
                dve.wait_ge(logit_done, s + 1)
                L = logit_ps[:, 0:TG * E].rearrange("p (t e) -> p t e", e=E)
                nc.vector.reduce_max(mx[:, :], L, AX.X).then_inc(rc, 1)
                dve.wait_ge(s_kept, s + 1)
                stat_tile(s, 0)
                dve.wait_ge(rc, ROUTE * g + 1)
                nc.vector.tensor_tensor(gap[:, g, :, :], L, over(mx[:, :], E), ALU.subtract).then_inc(gap_done, 1)
                stat_tile(s, 1)
                dve.wait_ge(gap_done, g + 1)
                nc.vector.scalar_tensor_tensor(out=key[:, :, :], in0=gap[:, g, :, :], scalar=0.0,
                                               in1=tile_cols(CF_DESC, TG, E), op0=ALU.is_equal, op1=ALU.mult).then_inc(rc, 1)
                stat_tile(s, 2)
                dve.wait_ge(rc, ROUTE * g + 2)
                nc.vector.reduce_max(kmx[:, :], key[:, :, :], AX.X).then_inc(rc, 1)
                stat_tile(s, 3)
                dve.wait_ge(rc, ROUTE * g + 3)
                nc.vector.tensor_tensor(oh[:, :, :].rearrange("p e t -> p t e"), key[:, :, :], over(kmx[:, :], E),
                                        ALU.is_equal).then_inc(rc, 1)
                mean_var(s)
                dve.wait_ge(rc, ROUTE * g + 4)
                nc.vector.tensor_tensor_scan(incl[:, :, :].rearrange("p e t -> p (e t)"), cf[:, CF_RESET:CF_RESET + E * TG],
                                             oh[:, :, :].rearrange("p e t -> p (e t)"), 0.0, ALU.mult, ALU.add).then_inc(incl_done, 1)

            def score_gap(g):
                if g == 0:
                    dve.wait_ge(rstd_done, BG)
                else:
                    dve.wait_ge(rstd_late, 2)
                nc.vector.tensor_tensor(sgap[:, :, :], gap[:, g, :, :], over(rstd[:, g * TG:(g + 1) * TG], E), ALU.mult).then_inc(sgap_done, 1)

            def by_expert(ap):
                return ap.rearrange("p e t -> p t e")

            def across(ap, n):
                return ap.unsqueeze(1).to_broadcast([P, n, ap.shape[1]])

            def lanes(g):
                nc.vector.tensor_tensor(ohB[:, :, :], ch[:, CH_COUNT:CH_TOKEN].rearrange("p (a t) -> p a t", t=TG),
                                        across(lane16[:, :], P), ALU.is_equal).then_inc(lanes_done, 1)

            def route_slots(g):
                if g == 0:
                    dve.wait_ge(ld_ch, 16)
                dve.wait_ge(rank_done, g + 1)
                nc.vector.tensor_tensor(rsel[:, :, :], route_ps[:, RANK:RANK + E * TG].rearrange("p (e t) -> p e t", t=TG),
                                        oh[:, :, :], ALU.mult).then_inc(rk, 1)
                nc.vector.tensor_scalar(cnt[:, 0, :], route_ps[:, COUNT:COUNT + E], float(P - 1), None, ALU.add).then_inc(bs, 1)
                dve.wait_ge(rk, RK * g + 1)
                with nc.allow_low_precision(reason="ranks are whole numbers below 2**24"):
                    nc.vector.reduce_sum(tok_rank[:, :], by_expert(rsel[:, :, :]), AX.X).then_inc(rk, 1)
                dve.wait_ge(bs, BS * g + 1)
                nc.vector.tensor_scalar(cnt[:, 1, :], cnt[:, 0, :], LOG_P, None, ALU.logical_shift_right).then_inc(bs, 1)
                dve.wait_ge(rk, RK * g + 2)
                nc.vector.tensor_scalar(lane[:, :], tok_rank[:, :], P - 1, None, ALU.bitwise_and).then_inc(rk, 1)
                dve.wait_ge(bs, BS * g + 2)
                nc.vector.tensor_tensor_scan(ends[:, :], cb[:, CB_ONES:CB_ONES + E], cnt[:, 1, :], 0.0, ALU.mult, ALU.add).then_inc(bs, 1)
                dve.wait_ge(rk, RK * g + 3)
                nc.vector.tensor_copy(lane16[:, :], lane[:, :]).then_inc(lane_ready, 1)
                dve.wait_ge(bs, BS * g + 3)
                nc.vector.tensor_tensor(base[:, :], ends[:, :], cnt[:, 1, :], ALU.subtract).then_inc(bs, 1)
                nc.vector.tensor_scalar(rtile[:, :], tok_rank[:, :], LOG_P, None, ALU.logical_shift_right).then_inc(bs, 1)
                dve.wait_ge(bs, BS * g + 5)
                nc.vector.tensor_tensor(bsel[:, :, :], over(base[:, :], TG), oh[:, :, :], ALU.mult).then_inc(bs, 1)
                dve.wait_ge(bs, BS * g + 6)
                nc.vector.reduce_sum(tok_base[:, :], by_expert(bsel[:, :, :]), AX.X).then_inc(bs, 1)
                dve.wait_ge(bs, BS * g + 7)
                with nc.allow_low_precision(reason="slot tiles are whole numbers below 2**11"):
                    nc.vector.tensor_tensor(tile_of[:, :], tok_base[:, :], rtile[:, :], ALU.add).then_inc(bs, 1)
                dve.wait_ge(bs, BS * g + 8)
                nc.vector.tensor_tensor(ohA[:, :, :], ch[:, CH_COUNT:CH_COUNT + SG * TG].rearrange("p (a t) -> p a t", t=TG),
                                        across(tile_of[:, :], SG), ALU.is_equal).then_inc(bs, 1)
                dve.wait_ge(lane_ready, g + 1)
                dve.wait_ge(bs, BS * g + 9)
                nc.vector.tensor_tensor(rhsA[:, :, :], ohA[:, :, :], ch[:, CH_TOKEN:CH_END].rearrange("p (a t) -> p a t", t=TG),
                                        ALU.mult).then_inc(rhs_ready, 1)

            def output_slots(g):
                nc.vector.scalar_tensor_tensor(out=slot[:, g, :], in0=tok_base[:, :], scalar=float(P), in1=tok_rank[:, :],
                                               op0=ALU.mult, op1=ALU.add).then_inc(slot_done, 1)

            def tile_experts(g):
                nc.vector.tensor_tensor(tcmp[:, :, :], tile_cols(CF_TILE_E, SG, E),
                                        ends[:, :].unsqueeze(1).to_broadcast([P, SG, E]), ALU.is_ge).then_inc(te, 1)
                dve.wait_ge(te, TILE_E * g + 1)
                nc.vector.reduce_sum(tsum[:, :], tcmp[:, :, :], AX.X).then_inc(te, 1)
                dve.wait_ge(te, TILE_E * g + 2)
                nc.vector.tensor_scalar(tsum[:, :], tsum[:, :], float(E - 1), None, ALU.min).then_inc(te, 1)
                dve.wait_ge(te, TILE_E * g + 3)
                nc.vector.tensor_copy(texp[:, g, SG:SG + 1], ends[:, E - 1:E])
                nc.vector.tensor_copy(texp[:, g, 0:SG], tsum[:, :]).then_inc(texp_done, 1)

            def gather_index(g):
                dve.wait_ge(table_done, g + 1)
                nc.vector.tensor_copy(gidx[:, g, :], route_ps[:, TABLE:TABLE + SG]).then_inc(gidx_done, 1)

            def scores(g):
                dve.wait_ge(sig_done, g + 1)
                nc.vector.reciprocal(rn_[:, :, :], sn_[:, :, :]).then_inc(sc, 1)
                dve.wait_ge(sc, 3 * g + 1)
                nc.vector.tensor_tensor(rn_[:, :, :], rn_[:, :, :], sp_[:, :, :], ALU.mult).then_inc(sc, 1)
                dve.wait_ge(sc, 3 * g + 2)
                nc.vector.reduce_sum(den[:, :], rn_[:, :, :], AX.X).then_inc(sc, 1)
                dve.wait_ge(sc, 3 * g + 3)
                nc.vector.reciprocal(score[:, g, :], den[:, :]).then_inc(score_done, 1)

            def experts(q):
                g, a = q // QG, 2 * (q % QG)
                if q % QG == 0:
                    dve.wait_ge(texp_done, g + 1)
                _, e = nc.values_load_multi_w_load_instructions(
                    texp[0:1, g, a:a + 4], engines=[mybir.EngineType.DVE], min_val=0, max_val=E - 1,
                    skip_runtime_bounds_check_because="VectorE takes the minimum with E - 1 of a count that is never negative")
                return {q: e[0:2], q + 1: e[2:4]}

            def copy_w1(q, e):
                if q == 2:
                    dve.wait_ge(ld_w1, 16)
                if q >= RING4:
                    dve.wait_ge(up_done, q - RING4 + 1)
                for j in range(2):
                    last = nc.vector.tensor_copy(w1x[:, q % RING4, j, :], w1[:, bass.ds(e[j] * H, H)])
                last.then_inc(w1x_done, 1)

            def add_b2(q, e):
                dve.wait_ge(down_done, q + 1)
                if q == 0:
                    dve.wait_ge(ld_b2, 16)
                for j in range(2):
                    last = nc.vector.tensor_tensor(osb[:, first_tile(q) + j, :], o_ps[q % 2][:, j * C:(j + 1) * C],
                                                   b2[:, bass.ds(e[j] * C, C)], ALU.add)
                last.then_inc(o_done, 1)

            def rest(g):
                with dve.If(used_tiles(mybir.EngineType.DVE, dve, g) > MAIN):
                    e = rest_experts(mybir.EngineType.DVE, g)
                    dve.wait_ge(up_done, Q)
                    dve.wait_ge(o_zeroed[g], 16)
                    for i in range(REST):
                        nc.vector.tensor_copy(w1x[:, 0, 0, :], w1[:, bass.ds(e[i] * H, H)]).then_inc(r_w1[g], 1)
                        dve.wait_ge(r_down[g], i + 1)
                        nc.vector.tensor_tensor(osb[:, g * SG + MAIN + i, :], o_ps[0][:, 0:C],
                                                b2[:, bass.ds(e[i] * C, C)], ALU.add).then_inc(r_o[g], 1)

            def combine(i):
                if i < B * TB:
                    if i % TG == 0:
                        dve.wait_ge(score_done, i // TG + 1)
                        dve.wait_ge(x1_done, B - 1)
                        dve.wait_ge(x1_dve, 2)
                    dve.wait_ge(og_done[i % 4], 16 * (i // 4 + 1))
                    nc.vector.scalar_tensor_tensor(out=og[:, i, :], in0=og[:, i, :], scalar=score[:, i // TG, i % TG:i % TG + 1],
                                                   in1=x1[:, i, :], op0=ALU.mult, op1=ALU.add).then_inc(res_done, 1)
                if 1 <= i <= B * TB:
                    dve.wait_ge(res_done, i)
                    nc.vector.bn_stats(st2[:, i - 1, :], og[:, i - 1, :]).then_inc(st2_done, 1)
                if i >= 2:
                    dve.wait_ge(st2_done, i - 1)
                    nc.vector.bn_aggr(mv2[:, i - 2, :], st2[:, i - 2, :]).then_inc(mv2_done, 1)

            def inverse2(n):
                a, b = NORM_TILES[n]
                dve.wait_ge(dev2_done, n + 1)
                nc.vector.reciprocal(rstd2[:, a:b], dev2[:, a:b]).then_inc(rstd2_done, 1)
                dve.wait_ge(rstd2_done, n + 1)
                if n < len(NORM_TILES) - 1:
                    nc.vector.scalar_tensor_tensor(out=nmr2[:, a:b], in0=mv2[:, a:b, 0], scalar=-1.0, in1=rstd2[:, a:b],
                                                   op0=ALU.mult, op1=ALU.mult).then_inc(nmr2_done, 1)
                else:
                    for t in range(a, b):
                        nc.vector.tensor_scalar(y[:, t, :], og[:, t, :], mv2[:, t, 0:1], rstd2[:, t:t + 1],
                                                ALU.subtract, ALU.mult).then_inc(y_last, 1)

            def late_variances(s):
                ts = slice(s * TB, (s + 2) * TB)
                dve.wait_ge(mv_done, s + 2)
                nc.vector.tensor_scalar(nmean[:, ts], mv[:, ts, 0], -1.0, None, ALU.mult)
                nc.vector.tensor_scalar(var1[:, ts], mv[:, ts, 1], LN_EPS, None, ALU.add).then_inc(var_late, 1)

            def normalize(t0, t1):
                for t in range(t0, t1):
                    last = nc.vector.tensor_scalar(x1[:, t, :], x1[:, t, :], mv[:, t, 0:1], rstd[:, t:t + 1], ALU.subtract, ALU.mult)
                last.then_inc(x1_dve, 1)

            router_weights()
            for s in range(B):
                candidate(s)
                if s == 0:
                    router_norms()
                if s >= LAG and s != BG + 1:
                    stats(s - LAG)
                if s == BG:
                    mean_var(s - LAG)
                    route_experts(0)
                    dve.wait_ge(rstd_done, 2)
                    normalize(TB // 2, TB)
                    route_slots(0)
                    lanes(0)
                    gather_index(0)
                    tile_experts(0)
                    output_slots(0)
                    score_gap(0)
                    gated(s)
                else:
                    gated(s)
                    if s >= LAG and s != BG + 1:
                        mean_var(s - LAG)
                    if s == B - 1:
                        late_variances(BG)
                scan(s)
                if s in VECTOR_ADDS:
                    add_input(s)
                if s == 0:
                    scale_router()
            stats(B - 2)
            mean_var(B - 2)
            route_experts(1)
            late_variances(BG + 2)
            e_in = experts(2)
            copy_w1(2, e_in[2])
            route_slots(1)
            e_of = experts(0)
            dve.wait_ge(rstd_late, 2)
            normalize((B - 1) * TB, B * TB)
            add_b2(0, e_of[0])
            copy_w1(3, e_in[3])
            lanes(1)
            gather_index(1)
            add_b2(1, e_of[1])
            e_in = experts(4)
            copy_w1(4, e_in[4])
            e_of = experts(2)
            for q in range(2, Q):
                if q + 3 < Q:
                    if (q + 3) % 2 == 0:
                        e_in = experts(q + 3)
                    copy_w1(q + 3, e_in[q + 3])
                if q > 2 and q % 2 == 0:
                    e_of = experts(q)
                add_b2(q, e_of[q])
                if q == 4:
                    tile_experts(1)
                    output_slots(1)
                if q == 6:
                    scores(0)
                    score_gap(1)
            for g in range(G):
                rest(g)
            for i in range(B * TB + 2):
                if i == TG:
                    scores(1)
                combine(i)
                if i - 2 in [b for a, b in NORM_TILES[:-1]]:
                    inverse2([b for a, b in NORM_TILES].index(i - 2))
            inverse2(len(NORM_TILES) - 1)


def kernel(L0_attn_x, L0_attn_Wz, L0_attn_bz, L0_attn_Wh, L0_attn_bh, L0_ffn_w_red, L0_ffn_wg, L0_ffn_W1, L0_ffn_b1,
           L0_ffn_W2, L0_ffn_b2):
    import numpy as np
    import ml_dtypes
    import concourse.bacc as bacc
    from concourse import mybir as mb
    from concourse.bass_utils import run_bass_kernel_spmd

    cf = np.zeros((P, CF_END), np.float32)
    cf[:, CF_IDENT:CF_IDENT + P] = np.eye(P)
    cf[:, CF_DESC:CF_RESET] = np.tile(np.arange(E, 0, -1), TG)
    cf[:, CF_RESET:CF_TILE_E] = np.tile(np.arange(TG) > 0, E)
    cf[:, CF_TILE_E:CF_END] = np.repeat(np.arange(SG), E)
    cb = np.zeros((P, CB_END), np.float32)
    cb[:, CB_BEFORE:CB_ONES] = np.where(np.arange(P)[:, None] < np.arange(P)[None, :], 0, -1)
    cb[:, CB_ONES:CB_END] = 1
    ch = np.zeros((P, CH_END), np.float16)
    ch[:, CH_COUNT:CH_TOKEN] = np.repeat(np.arange(P), TG)
    ch[:, CH_TOKEN:CH_END] = np.tile(P * np.arange(TG), SG)[None, :] + np.arange(P)[:, None]
    arrays = {
        "xT": np.ascontiguousarray(np.asarray(L0_attn_x).reshape(N, C).T),
        "gate_w": np.concatenate([np.asarray(L0_attn_Wz).T, np.asarray(L0_attn_Wh).T, np.asarray(L0_attn_bz).reshape(C, 1),
                                  np.asarray(L0_attn_bh).reshape(C, 1)], axis=1),
        "router_w": np.concatenate([np.asarray(L0_ffn_w_red).T, np.asarray(L0_ffn_wg).T], axis=1),
        "w1": np.asarray(L0_ffn_W1),
        "b1": np.ascontiguousarray(np.asarray(L0_ffn_b1).reshape(E * H // P, P).T),
        "w2": np.asarray(L0_ffn_W2),
        "b2": np.asarray(L0_ffn_b2),
        "cf": cf,
        "cb": cb.astype(ml_dtypes.bfloat16),
        "ch": ch,
    }
    nc = bacc.Bacc("TRN2", target_bir_lowering=False, num_devices=1)
    args = [nc.dram_tensor(f"{n}_dram", a.shape, mb.dt.from_np(a.dtype), kind="ExternalInput").ap() for n, a in arrays.items()]
    out = nc.dram_tensor("out_dram", (N, C), mb.dt.float32, kind="ExternalOutput").ap()
    build_mingru_top1_moe(nc, *args, out)
    r = run_bass_kernel_spmd(nc, [{f"{n}_dram": a for n, a in arrays.items()}], core_ids=[0])
    return r.results[0]["out_dram"].reshape(B, S, C)
```
